# Optimizing a Trainium2 kernel written in Bass

```python
import numpy as np
import jax
import jax.numpy as jnp

def _softmax(x, axis=-1):
    return jax.nn.softmax(x, axis=axis)

def _gelu(x):
    return jax.nn.gelu(x, approximate=True)

def _silu(x):
    return jax.nn.silu(x)

def _sigmoid(x):
    return jax.nn.sigmoid(x)

def _layernorm(x, axis=-1, eps=1e-05):
    m = jnp.mean(x, axis=axis, keepdims=True)
    v = jnp.var(x, axis=axis, keepdims=True)
    return (x - m) / jnp.sqrt(v + eps)

def _scatter_add(tgt, idx, src, axis=0):
    return tgt.at[idx].add(src)

def _segment_sum(src, seg, n):
    return jax.ops.segment_sum(src, seg, n)
kernel_name = 'mk_metaformer_d1_conv_nhwc768_r2_e43b19'

def setup_inputs(seed: int=0):
    np.random.seed(seed)
    _w = jnp.asarray

    def _rec_inputs():
        import jax
        import jax.numpy as jnp
        _gk = jax.random.key(seed)
        x = -0.0004039 + 1 * jax.random.normal(jax.random.fold_in(_gk, 1), (4, 32, 32, 384), jnp.float32)
        return x
    x = _rec_inputs()

    def _L0_conv_setup():
        import jax, jax.numpy as jnp
        import numpy as np
        B_, H_, W_, DM = (4, 32, 32, 384)
        DI = int(0.5 * DM)
        N = 16
        R = -(-DM // 16)
        K = 4

        def selective_scan(xs, dts, As, Bs, Cs, Dsk):
            u = jnp.moveaxis(xs, -1, 0)
            d = jnp.moveaxis(dts, -1, 0)
            Bt = jnp.moveaxis(Bs, -1, 0)
            Ct = jnp.moveaxis(Cs, -1, 0)

            def step(h, inp):
                u_t, d_t, B_t, C_t = inp
                dA = jnp.exp(d_t[..., None] * As)
                h = h * dA + (d_t * u_t)[..., None] * B_t[:, :, None, :]
                y = jnp.einsum('bkcn,bkn->bkc', h, C_t)
                return (h, y)
            h0 = jnp.zeros(u.shape[1:] + (As.shape[-1],), u.dtype)
            _, ys = jax.lax.scan(step, h0, (u, d, Bt, Ct))
            ys = jnp.moveaxis(ys, 0, -1)
            return ys + Dsk[None, :, :, None] * xs
        key = jax.random.key(seed)
        ks = jax.random.split(key, 8)
        s = lambda i, shape, sc=0.02: jax.random.normal(ks[i], shape, jnp.float32) * sc
        return dict(x=jax.random.normal(ks[0], (B_, H_, W_, DM), jnp.float32), in_proj_w=s(1, (2 * DI, DM)), conv_w=s(2, (DI, 1, 3, 3)), conv_b=jnp.zeros((DI,), jnp.float32), x_proj_w=s(3, (K, R + 2 * N, DI)), dt_projs_w=s(4, (K, DI, R)), dt_projs_b=s(5, (K, DI)), A_logs=jnp.log(jnp.tile(jnp.arange(1, N + 1, dtype=jnp.float32)[None, :], (K * DI, 1))), Ds=jnp.ones((K * DI,), jnp.float32), out_norm_g=jnp.ones((DI,), jnp.float32), out_norm_b=jnp.zeros((DI,), jnp.float32), out_proj_w=s(6, (DM, DI)))
    _L0_conv_all = _L0_conv_setup()
    _L0_conv_in = {k: v for k, v in _L0_conv_all.items() if k in ('in_proj_w', 'conv_w', 'conv_b', 'x_proj_w', 'dt_projs_w', 'dt_projs_b', 'A_logs', 'Ds', 'out_norm_g', 'out_norm_b', 'out_proj_w')}
    del _L0_conv_all

    def _L0_ffn_setup():
        import jax, jax.numpy as jnp
        import numpy as np
        NUM_EXPERT = 8
        TOP_K = 1
        key = jax.random.key(seed)
        ks = jax.random.split(key, 6)
        B, S, D, E, F = (8, 1024, 384, 8, 469)
        scale = 0.02
        return {'x': jax.random.normal(ks[0], (B, S, D), dtype=jnp.float32), 'Wg': jax.random.normal(ks[1], (E, D), dtype=jnp.float32) * scale, 'bg': jnp.zeros((E,), dtype=jnp.float32), 'W1': jax.random.normal(ks[2], (E, F, D), dtype=jnp.float32) * scale, 'W2': jax.random.normal(ks[3], (E, F, D), dtype=jnp.float32) * scale, 'W3': jax.random.normal(ks[4], (E, D, F), dtype=jnp.float32) * scale}
    _L0_ffn_all = _L0_ffn_setup()
    _L0_ffn_in = {k: v for k, v in _L0_ffn_all.items() if k in ('Wg', 'bg', 'W1', 'W2', 'W3')}
    del _L0_ffn_all
    return {'x': x, 'L0_conv_in_proj_w': _L0_conv_in['in_proj_w'], 'L0_conv_conv_w': _L0_conv_in['conv_w'], 'L0_conv_conv_b': _L0_conv_in['conv_b'], 'L0_conv_x_proj_w': _L0_conv_in['x_proj_w'], 'L0_conv_dt_projs_w': _L0_conv_in['dt_projs_w'], 'L0_conv_dt_projs_b': _L0_conv_in['dt_projs_b'], 'L0_conv_A_logs': _L0_conv_in['A_logs'], 'L0_conv_Ds': _L0_conv_in['Ds'], 'L0_conv_out_norm_g': _L0_conv_in['out_norm_g'], 'L0_conv_out_norm_b': _L0_conv_in['out_norm_b'], 'L0_conv_out_proj_w': _L0_conv_in['out_proj_w'], 'L0_ffn_Wg': _L0_ffn_in['Wg'], 'L0_ffn_bg': _L0_ffn_in['bg'], 'L0_ffn_W1': _L0_ffn_in['W1'], 'L0_ffn_W2': _L0_ffn_in['W2'], 'L0_ffn_W3': _L0_ffn_in['W3']}

def reference(x, L0_conv_in_proj_w, L0_conv_conv_w, L0_conv_conv_b, L0_conv_x_proj_w, L0_conv_dt_projs_w, L0_conv_dt_projs_b, L0_conv_A_logs, L0_conv_Ds, L0_conv_out_norm_g, L0_conv_out_norm_b, L0_conv_out_proj_w, L0_ffn_Wg, L0_ffn_bg, L0_ffn_W1, L0_ffn_W2, L0_ffn_W3):
    import jax
    import jax.numpy as jnp

    def _L0_conv_ref(x, in_proj_w, conv_w, conv_b, x_proj_w, dt_projs_w, dt_projs_b, A_logs, Ds, out_norm_g, out_norm_b, out_proj_w):
        import jax, jax.numpy as jnp
        import numpy as np
        B_, H_, W_, DM = (4, 32, 32, 384)
        DI = int(0.5 * DM)
        N = 16
        R = -(-DM // 16)
        K = 4

        def selective_scan(xs, dts, As, Bs, Cs, Dsk):
            u = jnp.moveaxis(xs, -1, 0)
            d = jnp.moveaxis(dts, -1, 0)
            Bt = jnp.moveaxis(Bs, -1, 0)
            Ct = jnp.moveaxis(Cs, -1, 0)

            def step(h, inp):
                u_t, d_t, B_t, C_t = inp
                dA = jnp.exp(d_t[..., None] * As)
                h = h * dA + (d_t * u_t)[..., None] * B_t[:, :, None, :]
                y = jnp.einsum('bkcn,bkn->bkc', h, C_t)
                return (h, y)
            h0 = jnp.zeros(u.shape[1:] + (As.shape[-1],), u.dtype)
            _, ys = jax.lax.scan(step, h0, (u, d, Bt, Ct))
            ys = jnp.moveaxis(ys, 0, -1)
            return ys + Dsk[None, :, :, None] * xs
        B, H, W, _ = x.shape
        L = H * W
        xz = x @ in_proj_w.T
        xh, z = jnp.split(xz, 2, axis=-1)
        xc = jnp.transpose(xh, (0, 3, 1, 2))
        xc = jax.lax.conv_general_dilated(xc, conv_w, (1, 1), 'SAME', feature_group_count=DI)
        xc = jax.nn.silu(xc + conv_b[None, :, None, None])
        x_flat = xc.reshape(B, DI, L)
        x_t = jnp.transpose(xc, (0, 1, 3, 2)).reshape(B, DI, L)
        x_hwwh = jnp.stack([x_flat, x_t], 1)
        xs = jnp.concatenate([x_hwwh, jnp.flip(x_hwwh, -1)], 1)
        x_dbl = jnp.einsum('bkdl,kcd->bkcl', xs, x_proj_w)
        dts, Bs, Cs = jnp.split(x_dbl, [R, R + N], axis=2)
        dts = jnp.einsum('bkrl,kdr->bkdl', dts, dt_projs_w)
        dts = jax.nn.softplus(dts + dt_projs_b[None, :, :, None])
        As = -jnp.exp(A_logs).reshape(K, DI, N)
        out_y = selective_scan(xs, dts, As, Bs, Cs, Ds.reshape(K, DI))
        inv_y = jnp.flip(out_y[:, 2:4], -1)
        wh_y = jnp.transpose(out_y[:, 1].reshape(B, DI, W, H), (0, 1, 3, 2)).reshape(B, DI, L)
        invwh_y = jnp.transpose(inv_y[:, 1].reshape(B, DI, W, H), (0, 1, 3, 2)).reshape(B, DI, L)
        y = out_y[:, 0] + inv_y[:, 0] + wh_y + invwh_y
        y = jnp.transpose(y, (0, 2, 1)).reshape(B, H, W, DI)
        mu = y.mean(-1, keepdims=True)
        var = y.var(-1, keepdims=True)
        y = (y - mu) / jnp.sqrt(var + 1e-05) * out_norm_g + out_norm_b
        y = y * jax.nn.silu(z)
        return y @ out_proj_w.T

    def _L0_ffn_ref(x, Wg, bg, W1, W2, W3):
        import jax, jax.numpy as jnp
        import numpy as np
        NUM_EXPERT = 8
        TOP_K = 1
        B, S, D = x.shape
        E = Wg.shape[0]
        xf = x.reshape(B * S, D)
        gate = xf @ Wg.T + bg
        vals, idx = jax.lax.top_k(gate, TOP_K)
        probs = jax.nn.softmax(vals, axis=-1)
        dispatch = jnp.sum(jax.nn.one_hot(idx, E, dtype=x.dtype) * probs[..., None], axis=1)
        h = jax.nn.silu(jnp.einsum('td,efd->tef', xf, W1)) * jnp.einsum('td,efd->tef', xf, W2)
        out = jnp.einsum('tef,edf,te->td', h, W3, dispatch)
        return out.reshape(B, S, D)

    def _gn(v, G=32, eps=1e-05):
        B_, H_, W_, C_ = v.shape
        g = v.reshape(B_, H_, W_, G, C_ // G)
        m = jnp.mean(g, axis=(1, 2, 4), keepdims=True)
        s = jnp.var(g, axis=(1, 2, 4), keepdims=True)
        return ((g - m) / jnp.sqrt(s + eps)).reshape(v.shape)

    def _ln_c(v, eps=1e-06):
        m = jnp.mean(v, axis=-1, keepdims=True)
        s = jnp.var(v, axis=-1, keepdims=True)
        return (v - m) / jnp.sqrt(s + eps)

    def _ln_t(v, eps=1e-05):
        m = jnp.mean(v, axis=-1, keepdims=True)
        s = jnp.var(v, axis=-1, keepdims=True)
        return (v - m) / jnp.sqrt(s + eps)

    def _to_tokens(v):
        B_, H_, W_, C_ = v.shape
        return v.reshape(B_, H_ * W_, C_)

    def _from_tokens(t, like):
        return t.reshape(like.shape)
    x = x + _L0_conv_ref(_ln_c(x), L0_conv_in_proj_w, L0_conv_conv_w, L0_conv_conv_b, L0_conv_x_proj_w, L0_conv_dt_projs_w, L0_conv_dt_projs_b, L0_conv_A_logs, L0_conv_Ds, L0_conv_out_norm_g, L0_conv_out_norm_b, L0_conv_out_proj_w)
    t = _to_tokens(x)
    t = t + _L0_ffn_ref(_ln_t(t), L0_ffn_Wg, L0_ffn_bg, L0_ffn_W1, L0_ffn_W2, L0_ffn_W3)
    x = _from_tokens(t, x)
    return x

_drawn_inputs = setup_inputs


def setup_inputs(seed=0):
    import zlib

    import numpy as np

    out = dict(_drawn_inputs(seed))
    spreads = {'L0_conv_conv_b': (0.0, 0.1),
     'L0_conv_Ds': (1.0, 0.6),
     'L0_conv_out_norm_g': (1.0, 0.6),
     'L0_conv_out_norm_b': (0.0, 0.8),
     'L0_ffn_bg': (0.0, 0.469)}
    factors = {'L0_conv_conv_w': 3.58,
     'L0_conv_x_proj_w': 64.0,
     'L0_conv_dt_projs_w': 64.0,
     'L0_conv_dt_projs_b': 200.0,
     'L0_conv_A_logs': 64.0}
    for name, (base, spread) in spreads.items():
        noise = np.random.default_rng([zlib.crc32(name.encode()), seed]).standard_normal(out[name].shape)
        drawn = base * np.exp(spread * noise) if base else spread * noise
        out[name] = jnp.asarray(drawn.astype(out[name].dtype))
    for name, factor in factors.items():
        out[name] = (out[name] * factor).astype(out[name].dtype)
    return out
```

```python
from contextlib import ExitStack

import concourse.bass as bass
from concourse import mybir

F32 = mybir.dt.float32
BF16 = mybir.dt.bfloat16
I32 = mybir.dt.int32
U32 = mybir.dt.uint32
ALU = mybir.AluOpType
ACT = mybir.ActivationFunctionType
AX_X = mybir.AxisListType.X

P = 128
NB, HH, WW, DM = 4, 32, 32, 384
L = HH * WW
DI, NS, R, ND = 192, 16, 24, 4
PAIRS = NB // 2
CG = 3
KC = DM // P
TT = L // P
HALF = 512
NE, F = 8, 469
FC = 4
TOK = NB * L
TILES = TOK // P
NT = TILES + NE
PW = WW + 2
U = 4
KORDER = (0, 2, 1, 3)
MAX_LOG = 80.5
F_LAST = F - (FC - 1) * P


def build(nc, x, w_in, conv_w, conv_b, w_xd, w_dt, b_dt, a_log, d_skip, ln_g, ln_b, w_out,
          w_gate, b_gate, w1, w2, w3, sel, ident_d, half_ones, tri_d, out):
    ctx = ExitStack()
    with ctx:
        def sb(name, shape, dt=F32):
            return ctx.enter_context(nc.sbuf_tensor(name, shape, dt))

        def sem(name):
            return ctx.enter_context(nc.semaphore(name))

        z_dram = nc.dram_tensor("z_dram", [PAIRS, P, CG * L], F32, kind="Internal").ap()
        t_dram = nc.dram_tensor("t_dram", [NB, L, DM], F32, kind="Internal").ap()
        sorted_in = nc.dram_tensor("sorted_in", [NT * P, DM], F32, kind="Internal").ap()
        sorted_out = nc.dram_tensor("sorted_out", [NT * P, DM], F32, kind="Internal").ap()

        ident = sb("ident", [P, P])
        ones = sb("ones", [P, P])
        mean_w = sb("mean_w", [P, P])
        tri = sb("tri", [P, P])
        eps6 = sb("eps6", [P, 1])
        eps5 = sb("eps5", [P, 1])
        one = sb("one", [P, 1])
        spare = sb("spare", [P, 1])
        small = sb("small", [P, 16, 6])
        mv = sb("mv", [P, TILES, 2])
        rstd = sb("rstd", [P, TILES])
        slot_u = sb("slot_u", [P, TILES], U32)
        expert_i = sb("expert_i", [P, NT], I32)

        ARENA = 51400
        arena = sb("arena", [P, ARENA])
        top = [0]

        def carve(n):
            at = top[0]
            top[0] += n
            assert top[0] <= ARENA, top[0]
            return arena[:, at:at + n]

        GL = CG * L
        g3 = lambda ap: ap.rearrange("p (j l) -> p j l", j=CG)
        X = [carve(GL) for _ in range(U)]
        dA = [carve(GL) for _ in range(2)]
        delta = carve(GL)
        du = carve(GL)
        Bs = [carve(L) for _ in range(U)]
        Cs = [carve(L) for _ in range(U)]
        xc = carve(GL)
        xcT = carve(GL)
        yrow = carve(GL)
        xd = carve(L)
        stackB = carve(L // 2).bitcast(BF16)
        stackC = carve(L // 2).bitcast(BF16)
        wxd = carve(ND * CG * P).rearrange("p (k j m) -> p k j m", k=ND, j=CG)
        wdt = carve(ND * CG * P).rearrange("p (k j m) -> p k j m", k=ND, j=CG)
        diag = carve(ND * CG * P).rearrange("p (k j m) -> p k j m", k=ND, j=CG)
        selw = carve(NS * P // 2).bitcast(BF16).rearrange("p (n m) -> p n m", n=NS)
        A = carve(ND * CG * NS).rearrange("p (k j n) -> p k j n", k=ND, j=CG)
        cw = carve(CG * 9).rearrange("p (j t) -> p j t", j=CG)
        cb = carve(CG)
        bdt = carve(ND * CG).rearrange("p (k j) -> p k j", k=ND)
        dsk = carve(ND * CG).rearrange("p (k j) -> p k j", k=ND)
        lng = carve(CG)
        lnb = carve(CG)
        X3, dA3, delta3, du3 = [g3(t) for t in X], [g3(t) for t in dA], g3(delta), g3(du)
        xc3, xcT3, yrow3 = g3(xc), g3(xcT), g3(yrow)
        xin = [X[b].rearrange("p (t c) -> p t c", t=TT) for b in range(2)]
        xnT = [dA[b].rearrange("p (k l) -> p k l", k=KC) for b in range(2)]
        pad_at = 2 * GL
        padf = arena[:, pad_at:pad_at + CG * PW * PW]
        pad = padf.rearrange("p (j h w) -> p j h w", j=CG, h=PW)
        bs_at = 8 * GL
        win = arena[:, bs_at:bs_at + KC * DM].rearrange("p (k m) -> p k m", k=KC)
        cs_at = bs_at + U * L
        wout = arena[:, cs_at:cs_at + CG * DM].rearrange("p (j m) -> p j m", j=CG)
        zs, zs3 = du, du3
        acc3 = delta3
        res1 = X[0][:, 0:L]
        res2 = X[0][:, L:2 * L]
        sp_hi = X[0][:, 2 * L:2 * L + L // 2].bitcast(BF16)
        sp_mid = X[0][:, 2 * L + L // 2:3 * L].bitcast(BF16)
        sp_lo = X[3][:, 0:L // 2].bitcast(BF16)
        top[0] = 0
        W1 = carve(KC * NE * F).rearrange("p (k n) -> p k n", k=KC)
        W2 = carve(KC * NE * F).rearrange("p (k n) -> p k n", k=KC)
        W3 = carve(FC * NE * DM).rearrange("p (k n) -> p k n", k=FC)
        tn_at = top[0]
        tn = carve(TILES * DM).rearrange("p (t c) -> p t c", t=TILES)
        wg = carve(KC * NE).rearrange("p (k e) -> p k e", k=KC)
        bg = carve(NE)
        iota_n = carve(NT)
        rev = carve(NE)
        route_at = top[0]
        gate = carve(TILES * NE).rearrange("p (t e) -> p t e", t=TILES)
        hot = carve(TILES * NE).rearrange("p (t e) -> p t e", t=TILES)
        pre = carve(TILES * NE).rearrange("p (t e) -> p t e", t=TILES)
        best = carve(TILES)
        cnt = carve(NE)
        cnt_i = carve(NE).bitcast(I32)
        ends = carve(NE)
        base = carve(NE)
        slot = carve(TILES)
        cmp = carve(NE * NT).rearrange("p (n e) -> p n e", e=NE)
        ef = carve(NT)
        tnT = [carve(KC * P).rearrange("p (k m) -> p k m", k=KC) for _ in range(2)]
        top[0] = tn_at
        xs = [carve(DM) for _ in range(2)]
        xsT = [carve(KC * P).rearrange("p (k m) -> p k m", k=KC) for _ in range(2)]
        act1 = [carve(F) for _ in range(2)]
        hid = [carve(F) for _ in range(2)]
        hidT = [carve(FC * P).rearrange("p (k m) -> p k m", k=FC) for _ in range(2)]
        yo = [carve(DM) for _ in range(2)]
        top[0] = 0
        fin_y = carve(TILES * DM).rearrange("p (t c) -> p t c", t=TILES)
        fin_t = carve(TILES * DM).rearrange("p (t c) -> p t c", t=TILES)

        psum = ctx.enter_context(nc.psum_tensor("psum", [P, 8, HALF], F32))
        bank = [psum[:, i, :] for i in range(8)]
        Y3 = psum[:, 0:6, :].rearrange("p (j h) n -> p j (h n)", j=CG)

        def names(*ns):
            return [sem(n) for n in ns]

        (s_const, s_zero, s_setup, s_x, s_var, s_std, s_xn, s_xTps, s_xT, s_win, s_proj, s_xh, s_z,
         s_zst, s_pad, s_conv, s_xc) = names(
            "const_loaded", "zero_ready", "setup_done", "x_loaded", "var_ready", "std_ready", "xn_ready",
            "xT_in_psum", "xT_ready", "win_loaded", "proj_in_psum", "xh_ready", "z_ready", "z_stored",
            "pad_cleared", "conv_done", "xc_ready")
        (s_xdps, s_xd, s_split, s_stack, s_dtps, s_dt, s_sp, s_delta, s_du) = names(
            "xd_in_psum", "xd_ready", "split_ready", "stack_loaded", "dt_in_psum", "dt_read",
            "softplus_parts", "delta_ready", "du_ready")
        (s_bcps, s_bc, s_dA, s_dbu, s_scan, s_hc, s_xfree) = names(
            "bc_in_psum", "bc_ready", "dA_ready", "dbu_ready", "scan_done", "hc_ready", "x_slot_free")
        (s_y, s_yev, s_mean, s_yc, s_sq, s_var2, s_std2, s_yn, s_yg, s_zld, s_yz, s_wout, s_xr, s_ops, s_t,
         s_tst, s_pair) = names(
            "y_in_psum", "y_taken", "mean_in_psum", "yc_ready", "sq_ready", "var_in_psum", "std2_ready",
            "yn_ready", "yg_ready", "z_loaded", "yz_ready", "wout_loaded", "x_again", "out_in_psum",
            "t_ready", "t_stored", "pair_done")
        (s_vch, s_ach, s_gch, s_alog) = names("dve_chain", "act_chain", "pool_chain", "a_log_clamped")
        (s_wl, s_tl, s_rv, s_rs, s_tn, s_tTps, s_tT, s_gps, s_hot, s_cum, s_slot, s_scat, s_zf) = names(
            "weights_loaded", "t_loaded", "tvar_ready", "tstd_ready", "tn_ready", "tT_in_psum", "tT_ready",
            "gate_in_psum", "hot_ready", "counts_in_psum", "slots_ready", "scattered", "sorted_cleared")
        (s_xs, s_eTps, s_eT, s_h, s_sil, s_hid, s_hTps, s_hT, s_yps, s_yo, s_yst) = names(
            "xs_loaded", "xsT_in_psum", "xsT_ready", "hidden_in_psum", "silu_ready", "hidden_ready",
            "hiddenT_in_psum", "hiddenT_ready", "y_tile_in_psum", "y_tile_ready", "y_tile_stored")
        (s_gat, s_ft, s_add, s_out) = names("gathered", "t_again", "sum_ready", "out_stored")

        s_x, s_xr, s_xs, s_yst = ([s, sem(s.name + "_odd")] for s in (s_x, s_xr, s_xs, s_yst))
        s_gat = [s_gat] + [sem(f"gathered_{b}") for b in range(1, NB)]

        block = ctx.enter_context(nc.Block())
        ZERO_SRC = X[3][:, 0:DM]
        CREDIT_X = U
        HCREDIT = CG * 2
        VCH_PAIR = [0]

        def xw(t, kk):
            return xc3 if kk < 2 else xcT3

        @block.sync
        def _(sp):
            for dst, src in ((ident[:, :], ident_d), (mean_w[:, :], half_ones), (tri[:, :], tri_d),
                             (wxd, w_xd), (wdt[0:64], w_dt), (selw[0:96], sel), (A, a_log), (cw, conv_w),
                             (cb, conv_b), (bdt, b_dt), (dsk, d_skip), (lng, ln_g), (lnb, ln_b)):
                sp.dma_start(dst, src).then_inc(s_const, 16)
            sp.wait_ge(s_zero, 1)
            for n in range(NT):
                sp.dma_start(sorted_in[n * P:(n + 1) * P, :], ZERO_SRC).then_inc(s_zf, 16)
            sp.wait_ge(s_zf, 16 * NT)
            sp.wait_ge(s_setup, 3)
            with sp.Fori(0, PAIRS) as p:
                sp.dma_start(win, w_in).then_inc(s_win, 16)
                for b in range(2):
                    sp.dma_start(xin[b], x[bass.ds(p * 2 + b, 1)].rearrange("o (t q) c -> q (o t) c", q=P))\
                      .then_inc(s_x[b], 16)
                sp.wait_ge(s_z, p * 6 + 6)
                sp.dma_start(z_dram[bass.ds(p, 1)].rearrange("o q c -> (o q) c"), zs).then_inc(s_zst, 16)
                sp.wait_ge(s_zst, p * 16 + 16)
                for kk in range(ND):
                    sp.wait_ge(s_split, p * ND + kk + 1)
                    for r, part in enumerate((sp_hi, sp_mid, sp_lo)):
                        sp.dma_start(stackB[32 * r:32 * r + 32, :], part[64:96, :]).then_inc(s_stack, 16)
                        sp.dma_start(stackC[32 * r:32 * r + 32, :], part[96:128, :]).then_inc(s_stack, 16)
                sp.wait_ge(s_y, p * 2 + 2)
                sp.dma_start(wout, w_out).then_inc(s_wout, 16)
                sp.dma_start(zs, z_dram[bass.ds(p, 1)].rearrange("o q c -> (o q) c")).then_inc(s_zld, 16)
                for b in range(2):
                    sp.dma_start(dA[b].rearrange("p (t c) -> p t c", t=TT),
                                 x[bass.ds(p * 2 + b, 1)].rearrange("o (t q) c -> q (o t) c", q=P))\
                      .then_inc(s_xr[b], 16)
                for b in range(2):
                    sp.wait_ge(s_t, p * 16 + 8 * b + 8)
                    sp.dma_start(t_dram[bass.ds(p * 2 + b, 1)].rearrange("o (t q) c -> q (o t) c", q=P),
                                 dA[b].rearrange("p (t c) -> p t c", t=TT)).then_inc(s_tst, 16)
                sp.wait_ge(s_tst, p * 32 + 32)
                sp.sem_inc(s_pair, 1)

            sp.dma_start(wg, w_gate).then_inc(s_tl, 16)
            sp.dma_start(bg, b_gate.partition_broadcast(P)).then_inc(s_tl, 16)
            for b in range(NB):
                sp.dma_start(tn[:, b * TT:(b + 1) * TT, :], t_dram[b].rearrange("(t q) c -> q t c", q=P))\
                  .then_inc(s_tl, 16)
            for k in range(KC):
                sp.dma_start(W1[:, k, :], w1[k]).then_inc(s_wl, 16)
                sp.dma_start(W2[:, k, :], w2[k]).then_inc(s_wl, 16)
            for k in range(FC):
                sp.dma_start(W3[:, k, :], w3[k]).then_inc(s_wl, 16)
            sp.wait_ge(s_scat, 16 * TILES)

            def load_rows(n, u):
                sp.dma_start(xs[u], sorted_in[bass.ds(n * P, P), :]).then_inc(s_xs[u], 16)

            def store_rows(n, u):
                sp.wait_ge(s_yo, n + 1)
                sp.dma_start(sorted_out[bass.ds(n * P, P), :], yo[u]).then_inc(s_yst[u], 16)

            load_rows(0, 0)
            load_rows(1, 1)
            with sp.Fori(0, NT // 2 - 1) as i:
                for u in range(2):
                    n = i * 2 + u
                    sp.wait_ge(s_eTps, n + 1)
                    load_rows(n + 2, u)
                    store_rows(n, u)
            for u in range(2):
                store_rows(NT - 2 + u, u)
            for u in range(2):
                sp.wait_ge(s_yst[u], 16 * (NT // 2))
            sp.sem_inc(s_pair, 1)
            for b in range(NB):
                sp.dma_start(fin_t[:, b * TT:(b + 1) * TT, :], t_dram[b].rearrange("(t q) c -> q t c", q=P))\
                  .then_inc(s_ft, 16)
            for b in range(NB):
                sp.wait_ge(s_add, b + 1)
                sp.dma_start(out[b].rearrange("(t q) c -> q t c", q=P), fin_t[:, b * TT:(b + 1) * TT, :])\
                  .then_inc(s_out, 16)
            sp.wait_ge(s_out, 16 * NB)

        @block.gpsimd
        def _(g):
            g.memset(ZERO_SRC, 0.0).then_inc(s_zero, 1)
            g.memset(ones[:, :], 1.0).then_inc(s_gch, 1)
            g.sem_inc(s_hc, HCREDIT)
            g.wait_ge(s_const, 16 * 13)
            g.wait_ge(s_gch, 1)
            for k in range(ND):
                for j in range(CG):
                    last = g.tensor_scalar(diag[:, k, j, :], ident[:, :], dsk[:, k, j:j + 1], None, ALU.mult)
            last.then_inc(s_setup, 1)
            g.wait_ge(s_zf, 16 * NT)
            with g.Fori(0, PAIRS) as p:
                g.memset(padf, 0.0).then_inc(s_pad, 1)
                for kk in range(ND):
                    c = p * ND + kk

                    def times_c(n, u):
                        g.wait_ge(s_bc, c * (4 * NS) + n * 4 + 4)
                        for j in range(CG):
                            g.wait_ge(s_scan, c * (CG * NS) + n * CG + j + 1 + HCREDIT)
                            g.tensor_tensor(X3[u][:, j, :], X3[u][:, j, :], Cs[u], ALU.mult).then_inc(s_hc, 1)

                    with g.Fori(0, NS // U) as i:
                        for u in range(U):
                            times_c(i * U + u, u)
                g.wait_ge(s_yg, p * CG + CG)
                g.wait_ge(s_zld, p * 16 + 16)
                g.tensor_tensor(X[2], X[3], zs, ALU.mult).then_inc(s_yz, 1)
                g.wait_ge(s_pair, p + 1)
            g.iota(iota_n, [[1, NT]], base=0, channel_multiplier=0, allow_small_or_imprecise_dtypes=True)\
             .then_inc(s_gch, 1)
            g.iota(rev, [[-1, NE]], base=NE, channel_multiplier=0, allow_small_or_imprecise_dtypes=True)\
             .then_inc(s_gch, 1)
            g.wait_ge(s_slot, 1)
            g.wait_ge(s_tn, 1)
            for t in range(TILES):
                g.indirect_dma_start(sorted_in, bass.IndirectOffsetOnAxis(slot_u[:, t:t + 1], 0),
                                     tn[:, t, :], None).then_inc(s_scat, 16)
            g.wait_ge(s_pair, PAIRS + 1)
            for t in range(TILES):
                g.indirect_dma_start(fin_y[:, t, :], None, sorted_out,
                                     bass.IndirectOffsetOnAxis(slot_u[:, t:t + 1], 0)).then_inc(s_gat[t // TT], 16)

        @block.scalar
        def _(a):
            ach = [0]
            a.wait_ge(s_alog, 1)
            a.activation(A, A, ACT.Exp).then_inc(s_ach, 1)
            a.wait_ge(s_ach, 1)
            a.mul(A, A, -1.0).then_inc(s_setup, 1)
            with a.Fori(0, PAIRS) as p:
                a.wait_ge(s_var, p + 1)
                a.activation(rstd[:, 0:16], rstd[:, 0:16], ACT.Sqrt).then_inc(s_std, 1)
                for b in range(2):
                    for k in range(KC):
                        for h in range(2):
                            q = (b * KC + k) * 2 + h
                            a.wait_ge(s_xTps, p * 12 + q + 1)
                            a.activation(xnT[b][:, k, h * HALF:(h + 1) * HALF], bank[q % 2], ACT.Copy)\
                             .then_inc(s_xT, 1)
                for q in range(6):
                    a.wait_ge(s_proj, p * 12 + 6 + q + 1)
                    j, h = q // 2, q % 2
                    a.activation(zs3[:, j, h * HALF:(h + 1) * HALF], bank[2 + q], ACT.Silu).then_inc(s_z, 1)
                for j in range(CG):
                    a.wait_ge(s_conv, p * CG + j + 1)
                    a.activation(xc3[:, j, :], acc3[:, j, :], ACT.Silu).then_inc(s_xc, 1)
                for j in range(CG):
                    a.activation(xcT3[:, j, :].rearrange("p (w h) -> p w h", w=WW),
                                 acc3[:, j, :].rearrange("p (h w) -> p w h", w=WW), ACT.Silu).then_inc(s_xc, 1)
                a.preload_act_table_set("natural_log_exp_and_others")
                for kk in range(ND):
                    k = KORDER[kk]
                    c = p * ND + kk
                    for h in range(2):
                        a.wait_ge(s_xdps, c * 2 + h + 1)
                        a.activation(xd[:, h * HALF:(h + 1) * HALF], bank[6 + h], ACT.Copy).then_inc(s_xd, 1)
                    a.wait_ge(s_scan, c * (CG * NS) + HCREDIT)
                    for q in range(6):
                        j, h = q // 2, q % 2
                        cs = slice(h * HALF, (h + 1) * HALF)
                        a.wait_ge(s_dtps, c * 6 + q + 1)
                        a.activation(dA3[0][:, j, cs], bank[6 + q % 2], ACT.Abs, bias=bdt[:, k, j:j + 1])\
                         .then_inc(s_dt, 1)
                        a.activation(dA3[1][:, j, cs], bank[6 + q % 2], ACT.Relu, bias=bdt[:, k, j:j + 1])\
                         .then_inc(s_dt, 1)
                    a.wait_ge(s_dt, c * 12 + 12)
                    a.activation(dA[0], dA[0], ACT.Exp, scale=-1.0).then_inc(s_ach, 1)
                    a.wait_ge(s_ach, c * 1 + 2)
                    a.activation(delta, dA[0], ACT.Ln, bias=one[:, :]).then_inc(s_sp, 1)
                    a.wait_ge(s_delta, c + 1)
                    a.wait_ge(s_du, c + 1)

                    def copies(n, u):
                        a.wait_ge(s_dbu, c * NS + n + 1)
                        a.wait_ge(s_hc, c * (CG * NS) + n * CG + HCREDIT - CG * U + CG)
                        for h in range(2):
                            for i, dst in enumerate((Bs[u], Cs[u])):
                                a.wait_ge(s_bcps, c * (4 * NS) + n * 4 + 2 * h + i + 1)
                                a.activation(dst[:, h * HALF:(h + 1) * HALF], bank[6 + i], ACT.Copy)\
                                 .then_inc(s_bc, 1)

                    def first_copies(n, u):
                        for h in range(2):
                            for i, dst in enumerate((Bs[u], Cs[u])):
                                a.wait_ge(s_bcps, c * (4 * NS) + n * 4 + 2 * h + i + 1)
                                a.activation(dst[:, h * HALF:(h + 1) * HALF], bank[6 + i], ACT.Copy)\
                                 .then_inc(s_bc, 1)

                    def exps(n, u):
                        for j in range(CG):
                            a.wait_ge(s_scan, c * (CG * NS) + n * CG + j + 1)
                            a.activation(dA3[u % 2][:, j, :], delta3[:, j, :], ACT.Exp,
                                         scale=A[:, k, j, n:n + 1] if isinstance(n, int)
                                         else A[:, k, j, bass.ds(n, 1)]).then_inc(s_dA, 1)

                    first_copies(0, 0)
                    for u in range(U):
                        if u + 1 < U:
                            first_copies(u + 1, u + 1)
                        else:
                            a.wait_ge(s_dbu, c * NS + 1)
                            a.wait_ge(s_hc, c * (CG * NS) + CG + HCREDIT)
                            first_copies(U, 0)
                        exps(u, u)
                    with a.Fori(1, NS // U - 1) as i:
                        for u in range(U):
                            n = i * U + u
                            a.wait_ge(s_dbu, c * NS + n + 2 - U)
                            a.wait_ge(s_hc, c * (CG * NS) + (n + 2 - U) * CG + HCREDIT)
                            first_copies(n + 1, (u + 1) % U)
                            exps(n, u)
                    for u in range(U):
                        n = NS - U + u
                        if n + 1 < NS:
                            a.wait_ge(s_dbu, c * NS + n + 2 - U)
                            a.wait_ge(s_hc, c * (CG * NS) + (n + 2 - U) * CG + HCREDIT)
                            first_copies(n + 1, (u + 1) % U)
                        exps(n, u)
                    if kk == 1:
                        a.wait_ge(s_y, p * 2 + 1)
                        for j in range(CG):
                            a.activation(yrow3[:, j, :], Y3[:, j, :], ACT.Copy).then_inc(s_yev, 1)
                for h in range(2):
                    cs = slice(h * HALF, (h + 1) * HALF)
                    a.wait_ge(s_yc, p * 2 + h + 1)
                    a.activation(X3[1][:, :, cs], X3[0][:, :, cs], ACT.Square).then_inc(s_sq, 1)
                for h in range(2):
                    a.wait_ge(s_var2, p * 2 + h + 1)
                    a.activation(Bs[3][:, h * HALF:(h + 1) * HALF], bank[2 + h], ACT.Sqrt, bias=eps5[:, :])\
                     .then_inc(s_std2, 1)
                a.wait_ge(s_yn, p + 1)
                for j in range(CG):
                    a.activation(X3[3][:, j, :], X3[2][:, j, :], ACT.Identity, bias=lnb[:, j:j + 1],
                                 scale=lng[:, j:j + 1]).then_inc(s_yg, 1)
                a.wait_ge(s_pair, p + 1)
            a.wait_ge(s_rv, 1)
            a.activation(rstd[:, :], rstd[:, :], ACT.Sqrt).then_inc(s_rs, 1)
            for t in range(TILES):
                a.wait_ge(s_tTps, t + 1)
                if t >= 2:
                    a.wait_ge(s_gps, t - 1)
                a.activation(tnT[t % 2], bank[t % 2][:, 0:KC * P].rearrange("p (k m) -> p k m", k=KC), ACT.Copy)\
                 .then_inc(s_tT, 1)
            a.wait_ge(s_scat, 16 * TILES)

            def xsT_out(n, u):
                a.wait_ge(s_eTps, n + 1)
                a.activation(xsT[u], bank[0][:, 0:KC * P].rearrange("p (k m) -> p k m", k=KC), ACT.Copy)\
                 .then_inc(s_eT, 1)

            def silu(n, u):
                a.wait_ge(s_h, n + 1)
                a.activation(act1[u], bank[1 + u][:, 0:F], ACT.Silu).then_inc(s_sil, 1)

            xsT_out(0, 0)
            xsT_out(1, 1)
            a.preload_act_table(ACT.Silu)
            with a.Fori(0, NT // 2 - 1) as i:
                for u in range(2):
                    n = i * 2 + u
                    silu(n, u)
                    xsT_out(n + 2, u)
            silu(NT - 2, 0)
            silu(NT - 1, 1)

        @block.vector
        def _(v):
            chain = [0]
            first = [0]

            def link(ins, p=None):
                chain[0] += 1
                ins.then_inc(s_vch, 1)
                if p is None:
                    v.wait_ge(s_vch, chain[0])
                else:
                    v.wait_ge(s_vch, p * per_pair + chain[0])

            def body(p):
                for b in range(2):
                    v.wait_ge(s_x[b], p * 16 + 16)
                    for t in range(TT):
                        ins = v.bn_stats(small[:, b * TT + t, :], xin[b][:, t, :])
                link(ins, p)
                v.memset(spare[:, :], 0.0)
                for t in range(2 * TT):
                    ins = v.bn_aggr(mv[:, t, :], small[:, t, :])
                link(ins, p)
                v.tensor_scalar(rstd[:, 0:16], mv[:, 0:16, 1], 1e-6, None, ALU.add).then_inc(s_var, 1)
                v.wait_ge(s_std, p + 1)
                link(v.reciprocal(rstd[:, 0:16], rstd[:, 0:16]), p)
                for b in range(2):
                    for t in range(TT):
                        q = b * TT + t
                        ins = v.tensor_scalar(xin[b][:, t, :], xin[b][:, t, :], mv[:, q, 0:1],
                                              rstd[:, q:q + 1], ALU.subtract, ALU.mult)
                    ins.then_inc(s_xn, 1)
                v.wait_ge(s_pad, p + 1)
                for q in range(6):
                    j, h = q // 2, q % 2
                    v.wait_ge(s_proj, p * 12 + q + 1)
                    v.tensor_copy(pad[:, j, 1 + 16 * h:17 + 16 * h, 1:1 + WW],
                                  bank[2 + q].rearrange("p (h w) -> p h w", w=WW)).then_inc(s_xh, 1)
                v.wait_ge(s_xh, p * 6 + 6)
                for t in range(9):
                    dy, dx = t // 3, t % 3
                    if t:
                        v.wait_ge(s_vch, p * per_pair + chain[0])
                    for j in range(CG):
                        src = pad[:, j, dy:dy + HH, dx:dx + WW]
                        dst = acc3[:, j, :].rearrange("p (h w) -> p h w", w=WW)
                        if t == 0:
                            ins = v.tensor_scalar(dst, src, cw[:, j, 0:1], cb[:, j:j + 1], ALU.mult, ALU.add)
                        else:
                            ins = v.scalar_tensor_tensor(dst, src, cw[:, j, t:t + 1], dst, ALU.mult, ALU.add)
                        if t == 8:
                            ins.then_inc(s_conv, 1)
                    if t < 8:
                        chain[0] += 1
                        ins.then_inc(s_vch, 1)
                for kk in range(ND):
                    c = p * ND + kk
                    lo = slice(64, 128)
                    v.wait_ge(s_xd, c * 2 + 2)
                    v.wait_ge(s_xfree, c * NS + U)
                    link(v.tensor_copy(sp_hi[lo], xd[lo]), p)
                    link(v.tensor_tensor(res1[lo], xd[lo], sp_hi[lo], ALU.subtract), p)
                    link(v.tensor_copy(sp_mid[lo], res1[lo]), p)
                    link(v.tensor_tensor(res2[lo], res1[lo], sp_mid[lo], ALU.subtract), p)
                    v.tensor_copy(sp_lo[lo], res2[lo]).then_inc(s_split, 1)
                    v.wait_ge(s_sp, c + 1)
                    link(v.tensor_scalar(X[1], dA[0], 1.0, None, ALU.add), p)
                    link(v.scalar_tensor_tensor(X[2], X[1], -1.0, dA[0], ALU.add, ALU.subtract), p)
                    link(v.tensor_tensor(delta, delta, dA[1], ALU.add), p)
                    v.tensor_tensor(delta, delta, X[2], ALU.subtract).then_inc(s_delta, 1)
                    v.wait_ge(s_stack, c * 96 + 96)
                    v.wait_ge(s_delta, c + 1)
                    v.tensor_tensor(du, delta, (xc if kk < 2 else xcT), ALU.mult).then_inc(s_du, 1)
                    step = -1 if KORDER[kk] >= 2 else 1

                    def state(n, u):
                        if u == 0:
                            v.wait_ge(s_du, c + 1)
                        v.wait_ge(s_bc, c * (4 * NS) + n * 4 + 3)
                        v.wait_ge(s_xfree, c * NS + n + 1)
                        v.tensor_tensor(X3[u], du3, Bs[u][:, None, :].to_broadcast([P, CG, L]), ALU.mult)\
                         .then_inc(s_dbu, 1)
                        v.wait_ge(s_dbu, c * NS + n + 1)
                        for j in range(CG):
                            v.wait_ge(s_dA, c * (CG * NS) + n * CG + j + 1)
                            v.tensor_tensor_scan(X3[u][:, j, ::step], dA3[u % 2][:, j, ::step],
                                                 X3[u][:, j, ::step], 0.0, ALU.mult, ALU.add).then_inc(s_scan, 1)

                    with v.Fori(0, NS // U) as i:
                        for u in range(U):
                            state(i * U + u, u)
                v.wait_ge(s_y, p * 2 + 2)
                v.wait_ge(s_yev, p * 6 + 3)
                for j in range(CG):
                    v.tensor_tensor(yrow3[:, j, :].rearrange("p (h w) -> p h w", w=WW),
                                    Y3[:, j, :].rearrange("p (w h) -> p h w", w=WW),
                                    yrow3[:, j, :].rearrange("p (h w) -> p h w", w=WW), ALU.add)\
                     .then_inc(s_yev, 1)
                for h in range(2):
                    cs = slice(h * HALF, (h + 1) * HALF)
                    v.wait_ge(s_mean, p * 2 + h + 1)
                    v.tensor_tensor(X3[0][:, :, cs], yrow3[:, :, cs],
                                    bank[h][:, None, :].to_broadcast([P, CG, HALF]), ALU.subtract)\
                     .then_inc(s_yc, 1)
                for h in range(2):
                    v.wait_ge(s_std2, p * 2 + h + 1)
                    ins = v.reciprocal(xd[:, h * HALF:(h + 1) * HALF], Bs[3][:, h * HALF:(h + 1) * HALF])
                link(ins, p)
                v.tensor_tensor(X3[2], X3[0], xd[:, None, :].to_broadcast([P, CG, L]), ALU.mult).then_inc(s_yn, 1)
                for q in range(16):
                    b, t = q // TT, q % TT
                    if t == 0:
                        v.wait_ge(s_xr[b], p * 16 + 16)
                    tb = dA[b].rearrange("p (t c) -> p t c", t=TT)[:, t, :]
                    v.wait_ge(s_ops, p * 16 + q + 1)
                    v.tensor_tensor(tb, bank[4 + q % 4][:, 0:DM], tb, ALU.add).then_inc(s_t, 1)
                v.wait_ge(s_pair, p + 1)

            per_pair = 3 + 8 + ND * 7 + 1
            v.memset(eps5[:, :], 1e-5)
            v.memset(one[:, :], 1.0).then_inc(s_setup, 1)
            v.wait_ge(s_const, 16 * 13)
            v.tensor_scalar(A, A, MAX_LOG, None, ALU.min).then_inc(s_alog, 1)
            v.sem_inc(s_scan, HCREDIT)
            v.sem_inc(s_xfree, CREDIT_X)
            v.wait_ge(s_setup, 3)
            with v.Fori(0, PAIRS) as p:
                body(p)
            assert chain[0] == per_pair, (chain[0], per_pair)
            chain[0] = PAIRS * per_pair
            v.wait_ge(s_tl, 16 * (2 + NB))
            for half in range(2):
                for t in range(16):
                    ins = v.bn_stats(small[:, t, :], tn[:, half * 16 + t, :])
                link(ins)
                for t in range(16):
                    ins = v.bn_aggr(mv[:, half * 16 + t, :], small[:, t, :])
                link(ins)
            v.tensor_scalar(rstd[:, :], mv[:, :, 1], 1e-5, None, ALU.add).then_inc(s_rv, 1)
            v.wait_ge(s_rs, 1)
            link(v.reciprocal(rstd[:, :], rstd[:, :]))
            for t in range(TILES):
                v.tensor_scalar(tn[:, t, :], tn[:, t, :], mv[:, t, 0:1], rstd[:, t:t + 1],
                                ALU.subtract, ALU.mult).then_inc(s_tn, 1)
            v.wait_ge(s_gps, TILES)
            v.wait_ge(s_gch, 3)
            E3 = [P, TILES, NE]
            bc = lambda ap: ap[:, None, :].to_broadcast(E3)
            link(v.tensor_tensor(gate, bank[2][:, 0:TILES * NE].rearrange("p (t e) -> p t e", e=NE), bc(bg), ALU.add))
            link(v.tensor_reduce(best, gate, AX_X, ALU.max))
            link(v.tensor_tensor(hot, gate, best[:, :, None].to_broadcast(E3), ALU.is_equal))
            link(v.tensor_tensor(hot, hot, bc(rev), ALU.mult))
            link(v.tensor_reduce(best, hot, AX_X, ALU.max))
            v.tensor_tensor(hot, bc(rev), best[:, :, None].to_broadcast(E3), ALU.is_equal).then_inc(s_hot, 1)
            v.wait_ge(s_cum, 2)
            inside = bank[3][:, 0:TILES * NE].rearrange("p (t e) -> p t e", e=NE)
            totals = bank[4][:, 0:TILES * NE].rearrange("p (t e) -> p t e", e=NE)
            for e in range(NE):
                ins = v.tensor_tensor_scan(pre[:, :, e], ones[:, 0:TILES], totals[:, :, e], 0.0, ALU.mult, ALU.add)
            link(ins)
            link(v.tensor_scalar(cnt, pre[:, TILES - 1, :], float(P - 1), None, ALU.add))
            link(v.tensor_copy(cnt_i, cnt))
            link(v.tensor_scalar(cnt_i, cnt_i, 7, None, ALU.logical_shift_right))
            link(v.tensor_copy(cnt, cnt_i))
            link(v.tensor_tensor_scan(ends, ones[:, 0:NE], cnt, 0.0, ALU.mult, ALU.add))
            link(v.tensor_tensor(base, ends, cnt, ALU.subtract))
            link(v.tensor_scalar(base, base, float(P), None, ALU.mult))
            link(v.tensor_tensor(pre, pre, totals, ALU.subtract))
            link(v.tensor_tensor(pre, pre, inside, ALU.add))
            link(v.tensor_tensor(pre, pre, bc(base), ALU.add))
            link(v.tensor_tensor(pre, pre, hot, ALU.mult))
            link(v.tensor_reduce(slot, pre, AX_X, ALU.add))
            v.tensor_copy(slot_u[:, :], slot).then_inc(s_slot, 1)
            link(v.tensor_tensor(cmp, iota_n[:, :, None].to_broadcast([P, NT, NE]),
                                 ends[:, None, :].to_broadcast([P, NT, NE]), ALU.is_ge))
            link(v.tensor_reduce(ef, cmp, AX_X, ALU.add))
            link(v.tensor_scalar(ef, ef, float(NE - 1), None, ALU.min))
            v.tensor_copy(expert_i[:, :], ef).then_inc(s_slot, 1)
            v.wait_ge(s_scat, 16 * TILES)

            def gated(n, u):
                v.wait_ge(s_sil, n + 1)
                v.tensor_tensor(hid[u], act1[u], bank[3 + u][:, 0:F], ALU.mult).then_inc(s_hid, 1)

            def hidT_out(n, u):
                v.wait_ge(s_hTps, n + 1)
                v.tensor_copy(hidT[u][:, 0:FC - 1, :],
                              bank[5][:, 0:(FC - 1) * P].rearrange("p (k m) -> p k m", k=FC - 1)).then_inc(s_hT, 1)
                v.tensor_copy(hidT[u][0:F_LAST, FC - 1, :], bank[5][0:F_LAST, (FC - 1) * P:FC * P])\
                 .then_inc(s_hT, 1)

            def y_out(n, u, stored=None):
                v.wait_ge(s_yps, n + 1)
                if stored is not None:
                    v.wait_ge(s_yst[u], stored * 16)
                v.tensor_copy(yo[u], bank[6 + u][:, 0:DM]).then_inc(s_yo, 1)

            gated(0, 0)
            for n in (1, 2):
                gated(n, n % 2)
                hidT_out(n - 1, (n - 1) % 2)
                y_out(n - 1, (n - 1) % 2)
            with v.Fori(0, (NT - 4) // 2) as i:
                for w in range(2):
                    n = i * 2 + 3 + w
                    gated(n, (1 + w) % 2)
                    hidT_out(n - 1, w % 2)
                    y_out(n - 1, w % 2, i + 1)
            gated(NT - 1, 1)
            for n in (NT - 2, NT - 1):
                hidT_out(n, n % 2)
                y_out(n, n % 2, n // 2)
            for b in range(NB):
                v.wait_ge(s_ft, 16 * NB)
                v.wait_ge(s_gat[b], 16 * TT)
                sl = slice(b * TT, (b + 1) * TT)
                v.tensor_tensor(fin_t[:, sl, :], fin_t[:, sl, :], fin_y[:, sl, :], ALU.add).then_inc(s_add, 1)

        @block.tensor
        def _(t_):
            pe = t_
            pe.wait_ge(s_setup, 3)
            pe.wait_ge(s_const, 16 * 13)
            with pe.Fori(0, PAIRS) as p:
                for b in range(2):
                    pe.wait_ge(s_xn, p * 2 + b + 1)
                    for k in range(KC):
                        for h in range(2):
                            q = (b * KC + k) * 2 + h
                            if q >= 2:
                                pe.wait_ge(s_xT, p * 12 + q - 1)
                            for t in range(4):
                                ins = pe.transpose(bank[q % 2][:, t * P:(t + 1) * P],
                                                   xin[b][:, h * 4 + t, k * P:(k + 1) * P], ident[:, :])
                            ins.then_inc(s_xTps, 1)
                pe.wait_ge(s_xT, p * 12 + 12)
                pe.wait_ge(s_win, p * 16 + 16)
                for g in range(12):
                    j, h = g // 2, g % 2
                    if g >= 6:
                        pe.wait_ge(s_xh, p * 6 + g - 5)
                    for b in range(2):
                        for k in range(KC):
                            ins = pe.matmul(bank[2 + g % 6][64 * b:64 * b + 64, :],
                                            win[:, k, j * 64:(j + 1) * 64],
                                            xnT[b][:, k, h * HALF:(h + 1) * HALF], start=(k == 0), stop=(k == KC - 1))
                    ins.then_inc(s_proj, 1)
                for kk in range(ND):
                    k = KORDER[kk]
                    c = p * ND + kk
                    src = xc3 if kk < 2 else xcT3
                    if kk == 0:
                        pe.wait_ge(s_z, p * 6 + 6)
                        pe.wait_ge(s_xc, p * 6 + 3)
                    else:
                        pe.wait_ge(s_bc, c * (4 * NS))
                    if kk == 2:
                        pe.wait_ge(s_xc, p * 6 + 6)
                    for h in range(2):
                        for j in range(CG):
                            ins = pe.matmul(bank[6 + h], wxd[:, k, j, :], src[:, j, h * HALF:(h + 1) * HALF],
                                            start=(j == 0), stop=(j == CG - 1))
                        ins.then_inc(s_xdps, 1)
                    pe.wait_ge(s_xd, c * 2 + 2)
                    for q in range(6):
                        j, h = q // 2, q % 2
                        if q >= 2:
                            pe.wait_ge(s_dt, c * 12 + 2 * (q - 1))
                        pe.matmul(bank[6 + q % 2], wdt[0:64, k, j, :], xd[0:64, h * HALF:(h + 1) * HALF],
                                  start=True, stop=True).then_inc(s_dtps, 1)
                    if kk == 2:
                        pe.wait_ge(s_yev, p * 6 + 3)
                    for j in range(CG):
                        for h in range(2):
                            pe.matmul(Y3[:, j, h * HALF:(h + 1) * HALF], diag[:, k, j, :],
                                      src[:, j, h * HALF:(h + 1) * HALF], start=(kk % 2 == 0), stop=False,
                                      skip_group_check=True)
                    pe.wait_ge(s_dt, c * 12 + 12)
                    pe.wait_ge(s_stack, c * 96 + 96)

                    def spread(n, first_):
                        for h in range(2):
                            for i, st in enumerate((stackB, stackC)):
                                if not (first_ and h == 0):
                                    pe.wait_ge(s_bc, c * (4 * NS) + n * 4 + 2 * h + i - 1)
                                lhs = selw[0:96, n, :] if isinstance(n, int) else \
                                    selw[0:96, bass.ds(n, 1), :].rearrange("k o m -> k (o m)")
                                pe.matmul(bank[6 + i], lhs, st[0:96, h * HALF:(h + 1) * HALF],
                                          start=True, stop=True).then_inc(s_bcps, 1)

                    def sums(n, u, last=False):
                        for j in range(CG):
                            pe.wait_ge(s_hc, c * (CG * NS) + n * CG + j + 1 + HCREDIT)
                            for h in range(2):
                                ins = pe.matmul(Y3[:, j, h * HALF:(h + 1) * HALF], ident[:, :],
                                                X3[u][:, j, h * HALF:(h + 1) * HALF], start=False, stop=last,
                                                skip_group_check=True)
                        ins.then_inc(s_xfree, 1)
                        return ins

                    spread(0, True)
                    spread(1, False)
                    with pe.Fori(0, NS // U - 1) as i:
                        for u in range(U):
                            spread(i * U + u + 2, False)
                            sums(i * U + u, u)
                    for u in range(U):
                        n = NS - U + u
                        if n + 2 < NS:
                            spread(n + 2, False)
                        sums(n, u, last=(kk % 2 == 1 and u == U - 1))
                    if kk % 2 == 1:
                        pe.wait_ge(s_xfree, (c + 1) * NS + U)
                        pe.sem_inc(s_y, 1)
                pe.wait_ge(s_yev, p * 6 + 6)
                for rnd, (src_, done, ready) in enumerate(((yrow3, s_mean, s_yev), (X3[1], s_var2, s_sq))):
                    for h in range(2):
                        if rnd:
                            pe.wait_ge(s_sq, p * 2 + h + 1)
                        for j in range(CG):
                            ins = pe.matmul(bank[2 * rnd + h], mean_w[:, :], src_[:, j, h * HALF:(h + 1) * HALF],
                                            start=(j == 0), stop=(j == CG - 1))
                        ins.then_inc(done, 1)
                pe.wait_ge(s_yz, p + 1)
                pe.wait_ge(s_wout, p * 16 + 16)
                yz3 = X3[2]
                for q in range(16):
                    b, t = q // TT, q % TT
                    if q >= 4:
                        pe.wait_ge(s_t, p * 16 + q - 3)
                    for j in range(CG):
                        ins = pe.matmul(bank[4 + q % 4][:, 0:DM], yz3[64 * b:64 * b + 64, j, t * P:(t + 1) * P],
                                        wout[64 * b:64 * b + 64, j, :], start=(j == 0), stop=(j == CG - 1))
                    ins.then_inc(s_ops, 1)
                pe.wait_ge(s_pair, p + 1)
            pe.wait_ge(s_tl, 16 * (2 + NB))
            for t in range(TILES + 1):
                if t < TILES:
                    pe.wait_ge(s_tn, t + 1)
                    if t >= 2:
                        pe.wait_ge(s_tT, t - 1)
                    for k in range(KC):
                        ins = pe.transpose(bank[t % 2][:, k * P:(k + 1) * P], tn[:, t, k * P:(k + 1) * P], ident[:, :])
                    ins.then_inc(s_tTps, 1)
                if t >= 1:
                    n = t - 1
                    pe.wait_ge(s_tT, n + 1)
                    for k in range(KC):
                        ins = pe.matmul(bank[2][:, n * NE:(n + 1) * NE], tnT[n % 2][:, k, :], wg[:, k, :],
                                        start=(k == 0), stop=(k == KC - 1))
                    ins.then_inc(s_gps, 1)
            pe.wait_ge(s_hot, 1)
            hotf = hot.rearrange("p t e -> p (t e)")
            pe.matmul(bank[3][:, 0:TILES * NE], tri[:, :], hotf, start=True, stop=True).then_inc(s_cum, 1)
            pe.matmul(bank[4][:, 0:TILES * NE], ones[:, :], hotf, start=True, stop=True).then_inc(s_cum, 1)
            pe.wait_ge(s_slot, 2)
            pe.wait_ge(s_scat, 16 * TILES)
            pe.wait_ge(s_wl, 16 * (2 * KC + FC))

            def expert_of(n):
                at = expert_i[0:1, n:n + 1] if isinstance(n, int) else expert_i[0:1, bass.ds(n, 1)]
                return pe.value_load(at, min_val=0, max_val=NE - 1)

            def rows_T(n, u, rnd):
                pe.wait_ge(s_xs[u], rnd * 16 + 16)
                if not (isinstance(n, int) and n == 0):
                    pe.wait_ge(s_eT, n)
                for k in range(KC):
                    ins = pe.transpose(bank[0][:, k * P:(k + 1) * P], xs[u][:, k * P:(k + 1) * P], ident[:, :])
                ins.then_inc(s_eTps, 1)

            def hidden(n, u):
                e = expert_of(n)
                pe.wait_ge(s_eT, n + 1)
                if not (isinstance(n, int) and n < 2):
                    pe.wait_ge(s_hid, n - 1)
                for w, bk in ((W1, bank[1 + u]), (W2, bank[3 + u])):
                    for k in range(KC):
                        ins = pe.matmul(bk[:, 0:F], xsT[u][:, k, :], w[:, k, bass.ds(e * F, F)],
                                        start=(k == 0), stop=(k == KC - 1))
                ins.then_inc(s_h, 1)

            def hidden_T(n, u):
                pe.wait_ge(s_hid, n + 1)
                if not (isinstance(n, int) and n == 0):
                    pe.wait_ge(s_hT, n * 2)
                for k in range(FC):
                    m = P if k < FC - 1 else F_LAST
                    ins = pe.transpose(bank[5][0:m, k * P:(k + 1) * P], hid[u][:, k * P:k * P + m], ident[:, :])
                ins.then_inc(s_hTps, 1)

            def down(n, u):
                e = expert_of(n)
                pe.wait_ge(s_hT, n * 2 + 2)
                if not (isinstance(n, int) and n < 2):
                    pe.wait_ge(s_yo, n - 1)
                for k in range(FC):
                    m = P if k < FC - 1 else F_LAST
                    ins = pe.matmul(bank[6 + u][:, 0:DM], hidT[u][0:m, k, :], W3[0:m, k, bass.ds(e * DM, DM)],
                                    start=(k == 0), stop=(k == FC - 1))
                ins.then_inc(s_yps, 1)

            rows_T(0, 0, 0)
            rows_T(1, 1, 0)
            hidden(0, 0)
            for n in (1, 2):
                hidden(n, n % 2)
                hidden_T(n - 1, (n - 1) % 2)
                rows_T(n + 1, (n + 1) % 2, (n + 1) // 2)
                down(n - 1, (n - 1) % 2)
            with pe.Fori(0, (NT - 4) // 2) as i:
                for w in range(2):
                    n = i * 2 + 3 + w
                    hidden(n, (1 + w) % 2)
                    hidden_T(n - 1, w % 2)
                    rows_T(n + 1, w % 2, i + 2)
                    down(n - 1, w % 2)
            hidden(NT - 1, 1)
            hidden_T(NT - 2, 0)
            down(NT - 2, 0)
            hidden_T(NT - 1, 1)
            down(NT - 1, 1)


def kernel(**inputs):
    import ml_dtypes
    import numpy as np
    import concourse.bacc as _bacc
    from concourse.bass_utils import run_bass_kernel_spmd as _run

    a = {k.replace("L0_", ""): np.asarray(v) for k, v in inputs.items()}
    f4 = np.float32

    def both(v):
        v = v.reshape((CG, 64) + v.shape[1:])
        v = np.moveaxis(v, 1, 0)
        return np.ascontiguousarray(np.concatenate([v, v], axis=0))

    w_in = np.ascontiguousarray(a["conv_in_proj_w"].T.reshape(KC, P, 2 * DI).transpose(1, 0, 2))
    xp = a["conv_x_proj_w"]
    w_xd = np.zeros((P, ND, CG, P), f4)
    w_dt = np.zeros((64, ND, CG, P), f4)
    for k in range(ND):
        for j in range(CG):
            for b in range(2):
                rows = slice(64 * b, 64 * b + 64)
                ch = slice(64 * j, 64 * j + 64)
                w_xd[rows, k, j, 32 * b:32 * b + R] = xp[k, 0:R, ch].T
                w_xd[rows, k, j, 64 + 16 * b:80 + 16 * b] = xp[k, R:R + NS, ch].T
                w_xd[rows, k, j, 96 + 16 * b:112 + 16 * b] = xp[k, R + NS:, ch].T
                w_dt[32 * b:32 * b + R, k, j, rows] = a["conv_dt_projs_w"][k, ch, :].T
    sel = np.zeros((96, NS, P), ml_dtypes.bfloat16)
    for q in range(96):
        b, n = (q // 16) % 2, q % 16
        sel[q, n, 64 * b:64 * b + 64] = 1
    half_ones = np.zeros((P, P), f4)
    half_ones[0:64, 0:64] = 1.0 / DI
    half_ones[64:, 64:] = 1.0 / DI
    w3 = np.zeros((FC * P, NE * DM), f4)
    w3[0:F] = a["ffn_W3"].transpose(2, 0, 1).reshape(F, NE * DM)
    arrays = dict(
        x=np.ascontiguousarray(a["x"].reshape(NB, L, DM)),
        w_in=w_in,
        conv_w=both(a["conv_conv_w"].reshape(DI, 9)),
        conv_b=both(a["conv_conv_b"]),
        w_xd=w_xd, w_dt=w_dt,
        b_dt=np.ascontiguousarray(both(a["conv_dt_projs_b"].T).transpose(0, 2, 1)),
        a_log=np.ascontiguousarray(both(a["conv_A_logs"].reshape(ND, DI, NS).transpose(1, 0, 2)).transpose(0, 2, 1, 3)),
        d_skip=np.ascontiguousarray(both(a["conv_Ds"].reshape(ND, DI).T).transpose(0, 2, 1)),
        ln_g=both(a["conv_out_norm_g"]), ln_b=both(a["conv_out_norm_b"]),
        w_out=both(np.ascontiguousarray(a["conv_out_proj_w"].T)),
        w_gate=np.ascontiguousarray(a["ffn_Wg"].T.reshape(KC, P, NE).transpose(1, 0, 2)),
        b_gate=np.ascontiguousarray(a["ffn_bg"]),
        w1=np.ascontiguousarray(a["ffn_W1"].transpose(2, 0, 1).reshape(KC, P, NE * F)),
        w2=np.ascontiguousarray(a["ffn_W2"].transpose(2, 0, 1).reshape(KC, P, NE * F)),
        w3=w3.reshape(FC, P, NE * DM),
        sel=sel, ident_d=np.eye(P, dtype=f4), half_ones=half_ones,
        tri_d=np.triu(np.ones((P, P), f4), 1),
    )
    nc = _bacc.Bacc("TRN2", target_bir_lowering=False, num_devices=1)
    feed, aps = {}, {}
    for name, v in arrays.items():
        feed["in_" + name] = v
        aps[name] = nc.dram_tensor("in_" + name, v.shape, mybir.dt.from_np(v.dtype), kind="ExternalInput").ap()
    out = nc.dram_tensor("out_0", (NB, L, DM), F32, kind="ExternalOutput").ap()
    build(nc, **aps, out=out)
    r = _run(nc, [feed], core_ids=[0])
    return r.results[0]["out_0"].reshape(NB, HH, WW, DM)
```

```python
from contextlib import ExitStack

import concourse.bass as bass
from concourse import mybir

F32 = mybir.dt.float32
BF16 = mybir.dt.bfloat16
I32 = mybir.dt.int32
U32 = mybir.dt.uint32
ALU = mybir.AluOpType
ACT = mybir.ActivationFunctionType
AX_X = mybir.AxisListType.X

P = 128
NB, HH, WW, DM = 4, 32, 32, 384
L = HH * WW
DI, NS, R, ND = 192, 16, 24, 4
PAIRS = NB // 2
CG = 3
KC = DM // P
TT = L // P
HALF = 512
NE, F = 8, 469
FC = 4
TOK = NB * L
TILES = TOK // P
NT = TILES + NE
PW = WW + 2
U = 4
KORDER = (0, 2, 1, 3)
PREP = (2, 3, 0, 1)
ROW = DM + 3
MEAN, RSTD, NUM = DM, DM + 1, DM + 2
MAX_LOG = 80.5
F_LAST = F - (FC - 1) * P


def build(nc, x, w_in, conv_w, conv_b, w_xd, w_dt, bias_row, a_log, d_skip, ln_g, ln_b, w_out,
          w_gate, b_gate, w1, w2, w3, sel, ident_d, half_ones, tri_d, out):
    ctx = ExitStack()
    with ctx:
        def sb(name, shape, dt=F32):
            return ctx.enter_context(nc.sbuf_tensor(name, shape, dt))

        def sem(name):
            return ctx.enter_context(nc.semaphore(name))

        def sems(*ns):
            return [sem(n) for n in ns]

        z_dram = nc.dram_tensor("z_dram", [P, CG * L], F32, kind="Internal").ap()
        step_dram = nc.dram_tensor("step_dram", [2, 2, P, CG * L], F32, kind="Internal").ap()
        t_dram = nc.dram_tensor("t_dram", [P, 2 * TT * ROW], F32, kind="Internal").ap()
        sorted_in = nc.dram_tensor("sorted_in", [NT * P, ROW], F32, kind="Internal").ap()

        ident = sb("ident", [P, P])
        ones = sb("ones", [P, P])
        mean_w = sb("mean_w", [P, P])
        tri = sb("tri", [P, P])
        eps5 = sb("eps5", [P, 1])
        one = sb("one", [P, 1])
        small = sb("small", [P, 16, 6])
        mv = sb("mv", [P, 16, 2])
        rstd = sb("rstd", [P, 16])
        gate = sb("gate", [P, TILES, NE])
        wg = sb("wg", [P, KC, NE])
        bg = sb("bg", [P, NE])
        slot_u = sb("slot_u", [P, TILES], U32)
        expert_i = sb("expert_i", [P, NT], I32)

        ARENA = 51700
        arena = sb("arena", [P, ARENA])
        top = [0]

        def carve(n):
            at = top[0]
            top[0] += n
            assert top[0] <= ARENA, top[0]
            return arena[:, at:at + n]

        GL = CG * L
        g3 = lambda ap: ap.rearrange("p (j l) -> p j l", j=CG)
        X = [carve(GL) for _ in range(U)]
        dA = [carve(GL) for _ in range(2)]
        delta, du = [None] * 2, [None] * 2
        for i in range(2):
            delta[i], du[i] = carve(GL), carve(GL)
        Bs = [carve(L) for _ in range(U)]
        post_at = top[0]
        Cs = [carve(L) for _ in range(U)]
        stackB = [carve(L // 2).bitcast(BF16) for _ in range(ND)]
        stackC = [carve(L // 2).bitcast(BF16) for _ in range(ND)]
        y = carve(GL)
        xc_at = top[0]
        xc = carve(GL)
        late_at = top[0]
        selw = carve(NS * P // 2).bitcast(BF16).rearrange("p (n m) -> p n m", n=NS)
        A = carve(ND * CG * NS).rearrange("p (k j n) -> p k j n", k=ND, j=CG)
        wout = carve(CG * DM).rearrange("p (j m) -> p j m", j=CG)
        cw = carve(CG * 9).rearrange("p (j t) -> p j t", j=CG)
        cb = carve(CG)
        brow = carve(1)
        dsk = carve(ND * CG).rearrange("p (k j) -> p k j", k=ND)
        lng = carve(CG)
        lnb = carve(CG)
        zero_mm = carve(P // 2).bitcast(BF16)
        X3, dA3, delta3, du3 = ([g3(t) for t in ts_] for ts_ in (X, dA, delta, du))
        xc3, y3 = g3(xc), g3(y)
        xin = [X[b].rearrange("p (t c) -> p t c", t=TT) for b in range(2)]
        xnT = [dA[b].rearrange("p (k l) -> p k l", k=KC) for b in range(2)]
        padf = arena[:, 2 * GL:2 * GL + CG * PW * PW]
        pad = padf.rearrange("p (j h w) -> p j h w", j=CG, h=PW)
        acc3 = delta3[0]
        win = du[0][:, 0:KC * DM].rearrange("p (k m) -> p k m", k=KC)
        zs = arena[:, 10 * GL:11 * GL]
        zs3 = g3(zs)
        xcT, xcT3 = X[0], X3[0]
        E = [X[1], X[2]]
        one_e = X[3]
        xd = [dA[0][:, 0:L], dA[0][:, L:2 * L]]
        res = dA[0][:, 2 * L:3 * L]
        parts = [[dA[1][:, (3 * i + r) * (L // 2):(3 * i + r + 1) * (L // 2)].bitcast(BF16) for r in range(3)]
                 for i in range(2)]
        wxd = y[:, 0:CG * ND * P].rearrange("p (k j m) -> p k j m", k=ND, j=CG)
        wdt = y[:, CG * ND * P:2 * CG * ND * P].rearrange("p (k j m) -> p k j m", k=ND, j=CG)
        top[0] = post_at
        trow = carve(2 * TT * ROW).rearrange("p (t c) -> p t c", t=2 * TT)
        sq = trow.rearrange("p t c -> p (t c)")[:, TT * ROW:TT * ROW + GL]
        sq3 = g3(sq)
        std = carve(L)
        trow0_at = top[0]
        z2 = xc
        tn = [arena[:, xc_at + i * DM:xc_at + (i + 1) * DM] for i in range(4)]
        tnT = [arena[:, xc_at + (4 + i) * DM:xc_at + (5 + i) * DM].rearrange("p (k m) -> p k m", k=KC)
               for i in range(2)]
        top[0] = 0
        W1 = carve(KC * NE * F).rearrange("p (k n) -> p k n", k=KC)
        W2 = carve(KC * NE * F).rearrange("p (k n) -> p k n", k=KC)
        W3 = carve(FC * NE * DM).rearrange("p (k n) -> p k n", k=FC)
        assert top[0] <= post_at
        top[0] = trow0_at
        trow0f = carve(2 * TT * ROW)
        trow0 = trow0f.rearrange("p (t c) -> p t c", t=2 * TT)
        top[0] = max(top[0], late_at)
        iota_n = carve(NT)
        rev = carve(NE)
        hot = carve(TILES * NE).rearrange("p (t e) -> p t e", t=TILES)
        pre = carve(TILES * NE).rearrange("p (t e) -> p t e", t=TILES)
        best = carve(TILES)
        cnt = carve(NE)
        cnt_i = carve(NE).bitcast(I32)
        ends = carve(NE)
        base = carve(NE)
        slot = carve(TILES)
        cmp = carve(NE * NT).rearrange("p (n e) -> p n e", e=NE)
        ef = carve(NT)
        top[0] = post_at
        xs = [carve(ROW) for _ in range(4)]
        xn = [carve(DM) for _ in range(2)]
        xsT = [carve(KC * P).rearrange("p (k m) -> p k m", k=KC) for _ in range(2)]
        act1 = [carve(F) for _ in range(2)]
        hid = [carve(F) for _ in range(2)]
        hidT = [carve(FC * P).rearrange("p (k m) -> p k m", k=FC) for _ in range(2)]
        yo = [carve(DM) for _ in range(2)]
        pad_row = sb("pad_row", [P, ROW])
        gap = sb("gap", [P, 4])

        psum = ctx.enter_context(nc.psum_tensor("psum", [P, 8, HALF], F32))
        bank = [psum[:, i, :] for i in range(8)]
        Y3 = psum[:, 0:6, :].rearrange("p (j h) n -> p j (h n)", j=CG)
        V3 = [psum[:, 2 + 2 * j:4 + 2 * j, :].rearrange("p h n -> p (h n)") for j in range(CG)]

        s_const, s_consts2, s_padrow, s_setup, s_vset, s_alog = sems(
            "const_loaded", "late_const_loaded", "pad_row_ready", "setup_done", "dve_setup", "a_log_clamped")
        s_x = sems("x_loaded_0", "x_loaded_1")
        s_var, s_std, s_xn, s_xTps, s_xT, s_win, s_proj, s_xh, s_z, s_zst, s_pad, s_conv, s_xc = sems(
            "var_ready", "std_ready", "xn_ready", "xT_in_psum", "xT_ready", "win_loaded", "proj_in_psum",
            "xh_ready", "z_ready", "z_stored", "pad_cleared", "conv_done", "xc_ready")
        s_wprep, s_xdps, s_xd, s_hi, s_split, s_vps, s_e, s_ln, s_u, s_vread, s_delta, s_du = sems(
            "prep_weights", "xd_in_psum", "xd_ready", "hi_ready", "split_ready", "dt_in_psum", "exp_ready",
            "ln_ready", "one_plus_e_ready", "dt_read", "delta_ready", "du_ready")
        s_stack = sems("stack_loaded_0", "stack_loaded_1")
        s_stepst = sems("step_stored_0", "step_stored_1")
        s_steps = sems("step_loaded_0", "step_loaded_1")
        s_bcps, s_bc, s_dA, s_dbu, s_scan, s_hc, s_xfree = sems(
            "bc_in_psum", "bc_ready", "dA_ready", "dbu_ready", "scan_done", "hc_ready", "x_slot_free")
        s_yrow, s_skip, s_ysum, s_mean, s_yc, s_sq, s_var2, s_std2, s_yn, s_yg, s_zld, s_yz = sems(
            "y_row_taken", "skip_added", "y_summed", "mean_in_psum", "yc_ready", "sq_ready", "var_in_psum",
            "std2_ready", "yn_ready", "yg_ready", "z_loaded", "yz_ready")
        s_xr = sems("x_again_0", "x_again_1")
        s_ops, s_t, s_tv, s_ts, s_cols, s_num, s_tn, s_tTps, s_tT, s_gps, s_gate, s_tst = sems(
            "out_in_psum", "t_ready", "t_var_ready", "t_std_ready", "row_columns", "row_numbers", "tn_ready",
            "tnT_in_psum", "tnT_ready", "gate_in_psum", "gate_ready", "t_stored")
        s_vch, s_ach, s_gch = sems("dve_chain", "act_chain", "pool_chain")
        s_wl, s_t0, s_hot, s_cum, s_slot, s_scat, s_zf = sems(
            "expert_weights", "t0_loaded", "hot_ready", "counts_in_psum", "slots_ready", "scattered",
            "sorted_cleared")
        s_xs = [sem(f"xs_loaded_{i}") for i in range(4)]
        s_yst = sems("y_tile_stored_0", "y_tile_stored_1")
        s_gap, s_xnn, s_eTps, s_eT, s_h, s_sil, s_hid, s_hTps, s_hT, s_yps, s_yo = sems(
            "gap_written", "tile_normed", "xsT_in_psum", "xsT_ready", "hidden_in_psum", "silu_ready", "hidden_ready",
            "hiddenT_in_psum", "hiddenT_ready", "y_tile_in_psum", "y_tile_ready")

        C_BC, C_DBU, C_SCAN, C_HC, C_X = 2, U, 2 * CG, U * CG, U
        N_CONST = 17
        SN = CG * NS
        steps_of = lambda kk: kk % 2

        block = ctx.enter_context(nc.Block())

        @block.sync
        def _(sp):
            def load_x(p):
                for b in range(2):
                    sp.dma_start(xin[b], x[2 * p + b].rearrange("(t q) c -> q t c", q=P)).then_inc(s_x[b], 16)
                sp.dma_start(win, w_in).then_inc(s_win, 16)

            sp.dma_start(xin[0], x[0].rearrange("(t q) c -> q t c", q=P)).then_inc(s_x[0], 16)
            sp.dma_start(ident[:, :], ident_d).then_inc(s_const, 16)
            sp.dma_start(xin[1], x[1].rearrange("(t q) c -> q t c", q=P)).then_inc(s_x[1], 16)
            sp.dma_start(win, w_in).then_inc(s_win, 16)
            for dst, src in ((mean_w[:, :], half_ones), (tri[:, :], tri_d), (selw[0:96], sel), (A, a_log),
                             (cw, conv_w), (cb, conv_b), (brow, bias_row), (dsk, d_skip), (lng, ln_g),
                             (lnb, ln_b), (wout, w_out), (wg[:, :, :], w_gate),
                             (bg[:, :], b_gate.partition_broadcast(P))):
                sp.dma_start(dst, src).then_inc(s_const, 16)

            for p in range(PAIRS):
                if p:
                    sp.wait_ge(s_ops, 16 * p)
                sp.dma_start(wxd, w_xd).then_inc(s_wprep, 16)
                sp.dma_start(wdt[0:64], w_dt).then_inc(s_wprep, 16)
                sp.wait_ge(s_z, 6 * (p + 1))
                if p:
                    sp.wait_ge(s_zld, 16 * p)
                    sp.wait_ge(s_tst, 16)
                sp.dma_start(z_dram, zs).then_inc(s_zst, 16)

                def store_steps(i):
                    sp.wait_ge(s_du, ND * p + i + 1)
                    sp.dma_start(step_dram[i, 0], delta[i]).then_inc(s_stepst[i], 16)
                    sp.dma_start(step_dram[i, 1], du[i]).then_inc(s_stepst[i], 16)

                for i, kk in enumerate(PREP):
                    sp.wait_ge(s_split, ND * p + i + 1)
                    for r, part in enumerate(parts[i % 2]):
                        sp.dma_start(stackB[kk][32 * r:32 * r + 32, :], part[64:96, :]).then_inc(s_stack[i % 2], 16)
                        sp.dma_start(stackC[kk][32 * r:32 * r + 32, :], part[96:128, :]).then_inc(s_stack[i % 2], 16)
                    if i in (1, 2):
                        store_steps(i - 1)
                for i in range(2):
                    sp.wait_ge(s_scan, (ND * p + i + 1) * SN + C_SCAN)
                    sp.wait_ge(s_stepst[i], 32 * (p + 1))
                    sp.dma_start(delta[i], step_dram[i, 0]).then_inc(s_steps[i], 16)
                    sp.dma_start(du[i], step_dram[i, 1]).then_inc(s_steps[i], 16)
                sp.wait_ge(s_xfree, ND * NS * (p + 1) + C_X)

                def x_again(b):
                    sp.dma_start(trow[:, b * TT:(b + 1) * TT, 0:DM],
                                 x[2 * p + b].rearrange("(t q) c -> q t c", q=P)).then_inc(s_xr[b], 16)

                x_again(0)
                sp.wait_ge(s_skip, p + 1)
                sp.wait_ge(s_zst, 16 * (p + 1))
                sp.dma_start(z2, z_dram).then_inc(s_zld, 16)
                if p + 1 < PAIRS:
                    load_x(p + 1)
                sp.wait_ge(s_var2, 2 * (p + 1))
                x_again(1)
                if p + 1 < PAIRS:
                    sp.wait_ge(s_cols, p + 1)
                    sp.wait_ge(s_num, p + 1)
                    sp.dma_start(t_dram, trow.rearrange("q t c -> q (t c)")).then_inc(s_tst, 16)
            for k in range(KC):
                sp.dma_start(W1[:, k, :], w1[k]).then_inc(s_wl, 16)
            sp.wait_ge(s_gps, 16 * PAIRS)
            sp.dma_start(trow0f, t_dram).then_inc(s_t0, 16)
            for k in range(KC):
                sp.dma_start(W2[:, k, :], w2[k]).then_inc(s_wl, 16)
            for k in range(FC):
                sp.dma_start(W3[:, k, :], w3[k]).then_inc(s_wl, 16)
            sp.wait_ge(s_scat, 16 * TILES)

            def load_rows(n, slot_):
                sp.dma_start(xs[slot_], sorted_in[bass.ds(n * P, P), :]).then_inc(s_xs[slot_], 16)

            for n in range(4):
                load_rows(n, n)
            with sp.Fori(0, NT // 4 - 1) as i:
                for w in range(4):
                    sp.wait_ge(s_yst[w % 2], i * 32 + 16 * (w // 2 + 1))
                    load_rows(i * 4 + w + 4, w)

        @block.gpsimd
        def _(g):
            g.memset(pad_row[:, 0:NUM], 0.0).then_inc(s_gch, 1)
            g.iota(pad_row[:, NUM:NUM + 1].bitcast(I32), [[0, 1]], base=TOK, channel_multiplier=0).then_inc(s_gch, 1)
            g.memset(padf, 0.0).then_inc(s_pad, 1)
            g.memset(ones[:, :], 1.0)
            g.memset(zero_mm, 0.0).then_inc(s_setup, 1)
            g.sem_inc(s_hc, C_HC)
            g.sem_inc(s_gap, 4)
            g.wait_ge(s_gch, 2)
            for n in range(NT):
                g.dma_start(sorted_in[n * P:(n + 1) * P, :], pad_row[:, :]).then_inc(s_zf, 16)
            for p in range(PAIRS):
                if p:
                    g.memset(padf, 0.0).then_inc(s_pad, 1)
                for i, kk in enumerate(PREP):
                    c = ND * p + i
                    g.wait_ge(s_delta, c + 1)
                    g.tensor_tensor(du[i % 2], delta[i % 2], xc if kk < 2 else xcT, ALU.mult).then_inc(s_du, 1)
                for kk in range(ND):
                    c = ND * p + kk
                    with g.Fori(0, NS // U) as i:
                        for u in range(U):
                            n = i * U + u
                            g.wait_ge(s_bc, n * 4 + (c * 4 * NS + 4 + C_BC))
                            for j in range(CG):
                                g.wait_ge(s_scan, n * CG + (c * SN + j + 1 + C_SCAN))
                                g.tensor_tensor(X3[u][:, j, :], X3[u][:, j, :], Cs[u], ALU.mult)\
                                 .then_inc(s_hc, 1)
                g.wait_ge(s_var2, 2 * (p + 1))
                g.iota(trow[:, :, NUM].bitcast(I32), [[P, 2 * TT]], base=p * 2 * L, channel_multiplier=1)\
                 .then_inc(s_num, 1)
                g.wait_ge(s_zld, 16 * (p + 1))
                for j in range(CG):
                    g.wait_ge(s_yg, CG * p + j + 1)
                    g.tensor_tensor(y3[:, j, :], y3[:, j, :], g3(z2)[:, j, :], ALU.mult).then_inc(s_yz, 1)
            g.iota(iota_n, [[1, NT]], base=0, channel_multiplier=0, allow_small_or_imprecise_dtypes=True)\
             .then_inc(s_gch, 1)
            g.iota(rev, [[-1, NE]], base=NE, channel_multiplier=0, allow_small_or_imprecise_dtypes=True)\
             .then_inc(s_gch, 1)
            g.wait_ge(s_zf, 16 * NT)
            g.wait_ge(s_slot, 1)
            g.wait_ge(s_cols, PAIRS)
            for t in range(2 * TT, TILES):
                g.indirect_dma_start(sorted_in, bass.IndirectOffsetOnAxis(slot_u[:, t:t + 1], 0),
                                     trow[:, t - 2 * TT, :], None).then_inc(s_scat, 16)
            g.wait_ge(s_t0, 16)
            for t in range(2 * TT):
                g.indirect_dma_start(sorted_in, bass.IndirectOffsetOnAxis(slot_u[:, t:t + 1], 0),
                                     trow0[:, t, :], None).then_inc(s_scat, 16)

            def store_rows(n, slot_):
                g.wait_ge(s_gap, n + 1)
                g.wait_ge(s_yo, n + 1)
                g.tensor_tensor(gap[:, slot_:slot_ + 1], one[:, :], one[:, :], ALU.mult).then_inc(s_gap, 1)
                g.indirect_dma_start(out, bass.IndirectOffsetOnAxis(xs[slot_][:, NUM:NUM + 1].bitcast(U32), 0),
                                     yo[slot_ % 2], None, bounds_check=TOK - 1, oob_is_err=False)\
                 .then_inc(s_yst[slot_ % 2], 16)

            with g.Fori(0, NT // 4) as i:
                for w in range(4):
                    store_rows(i * 4 + w, w)
            for u in range(2):
                g.wait_ge(s_yst[u], 16 * (NT // 2))

        @block.scalar
        def _(a):
            count = [0]

            def own(ins):
                count[0] += 1
                ins.then_inc(s_ach, 1)
                a.wait_ge(s_ach, count[0])

            a.sem_inc(s_bc, C_BC)
            for p in range(PAIRS):
                a.wait_ge(s_var, p + 1)
                a.activation(rstd[:, :], rstd[:, :], ACT.Sqrt).then_inc(s_std, 1)
                for b in range(2):
                    for k in range(KC):
                        for h in range(2):
                            q = (b * KC + k) * 2 + h
                            a.wait_ge(s_xTps, p * 12 + q + 1)
                            a.activation(xnT[b][:, k, h * HALF:(h + 1) * HALF], bank[q % 2], ACT.Copy)\
                             .then_inc(s_xT, 1)
                for q in range(6):
                    a.wait_ge(s_proj, p * 12 + 6 + q + 1)
                    j, h = q // 2, q % 2
                    a.activation(zs3[:, j, h * HALF:(h + 1) * HALF], bank[2 + q], ACT.Silu).then_inc(s_z, 1)
                if p:
                    a.wait_ge(s_gps, 16 * p)
                for j in range(CG):
                    a.wait_ge(s_conv, p * CG + j + 1)
                    a.activation(xcT3[:, j, :].rearrange("p (w h) -> p w h", w=WW),
                                 acc3[:, j, :].rearrange("p (h w) -> p w h", w=WW), ACT.Silu).then_inc(s_xc, 1)
                for j in range(CG):
                    a.activation(xc3[:, j, :], acc3[:, j, :], ACT.Silu).then_inc(s_xc, 1)
                a.preload_act_table_set("natural_log_exp_and_others")
                if p == 0:
                    a.wait_ge(s_alog, 1)
                    own(a.activation(A, A, ACT.Exp))
                    own(a.mul(A, A, -1.0))
                a.wait_ge(s_xc, 6 * (p + 1))
                for i, kk in enumerate(PREP):
                    c = ND * p + i
                    par = i % 2
                    if i >= 2:
                        a.wait_ge(s_vps, 3 * (c - 1))
                        a.wait_ge(s_split, c - 1)
                        a.wait_ge(s_stack[par], 96 * (2 * p + 1))
                    for h in range(2):
                        cs = slice(h * HALF, (h + 1) * HALF)
                        a.wait_ge(s_xdps, 2 * c + h + 1)
                        a.activation(xd[par][:, cs], bank[h], ACT.Identity, bias=brow).then_inc(s_xd, 1)
                        a.activation(parts[par][0][64:128, cs], bank[h][64:128, :], ACT.Copy).then_inc(s_hi, 1)
                    if i >= 2:
                        a.wait_ge(s_delta, c - 1)
                        a.wait_ge(s_stepst[par], 32 * (p + 1))
                    for j in range(CG):
                        a.wait_ge(s_vps, 3 * c + j + 1)
                        ins = a.activation(g3(E[par])[:, j, :], V3[j], ACT.Abs)
                    own(ins)
                    a.activation(E[par], E[par], ACT.Exp, scale=-1.0).then_inc(s_e, 1)
                    a.wait_ge(s_e, c + 1)
                    if i:
                        a.wait_ge(s_delta, c)
                    a.activation(one_e, E[par], ACT.Identity, bias=one[:, :]).then_inc(s_u, 1)
                    a.activation(delta[par], E[par], ACT.Ln, bias=one[:, :]).then_inc(s_ln, 1)

                def copies(kk, n, u):
                    c = ND * p + kk
                    a.wait_ge(s_dbu, n + (c * NS + 1 - U + C_DBU))
                    a.wait_ge(s_hc, n * CG + (c * SN + CG - U * CG + C_HC))
                    for h in range(2):
                        for q, dst in enumerate((Bs[u], Cs[u])):
                            a.wait_ge(s_bcps, n * 4 + (c * 4 * NS + 2 * h + q + 1))
                            a.activation(dst[:, h * HALF:(h + 1) * HALF], bank[6 + q], ACT.Copy).then_inc(s_bc, 1)

                def exps(kk, n, u):
                    c = ND * p + kk
                    for j in range(CG):
                        a.wait_ge(s_scan, n * CG + (c * SN + j + 1 - 2 * CG + C_SCAN))
                        a.activation(dA3[u % 2][:, j, :], delta3[steps_of(kk)][:, j, :], ACT.Exp,
                                     scale=A[:, KORDER[kk], j, n:n + 1] if isinstance(n, int)
                                     else A[:, KORDER[kk], j, bass.ds(n, 1)]).then_inc(s_dA, 1)

                a.wait_ge(s_zst, 16 * (p + 1))
                a.wait_ge(s_du, ND * (p + 1))
                a.wait_ge(s_stack[0], 192 * (p + 1))
                a.wait_ge(s_stack[1], 192 * (p + 1))
                copies(0, 0, 0)
                for kk in range(ND):
                    if kk >= 2:
                        a.wait_ge(s_steps[kk - 2], 32 * (p + 1))
                    for u in range(U):
                        exps(kk, u, u)
                        if kk == 2 and u == 0:
                            a.wait_ge(s_xfree, (ND * p + 2) * NS + C_X)
                            for j in range(CG):
                                a.activation(y3[:, j, :], Y3[:, j, :], ACT.Copy).then_inc(s_yrow, 1)
                        copies(kk, u + 1, (u + 1) % U)
                    with a.Fori(1, NS // U - 1) as i:
                        for u in range(U):
                            exps(kk, i * U + u, u)
                            copies(kk, i * U + u + 1, (u + 1) % U)
                    for u in range(U):
                        n = NS - U + u
                        exps(kk, n, u)
                        if n + 1 < NS:
                            copies(kk, n + 1, (u + 1) % U)
                        elif kk + 1 < ND:
                            copies(kk + 1, 0, 0)
                for h in range(2):
                    cs = slice(h * HALF, (h + 1) * HALF)
                    a.wait_ge(s_yc, 2 * p + h + 1)
                    a.activation(sq3[:, :, cs], y3[:, :, cs], ACT.Square).then_inc(s_sq, 1)
                for h in range(2):
                    a.wait_ge(s_var2, 2 * p + h + 1)
                    a.activation(std[:, h * HALF:(h + 1) * HALF], bank[2 + h], ACT.Sqrt, bias=eps5[:, :])\
                     .then_inc(s_std2, 1)
                for j in range(CG):
                    a.wait_ge(s_yn, CG * p + j + 1)
                    a.activation(y3[:, j, :], y3[:, j, :], ACT.Identity, bias=lnb[:, j:j + 1],
                                 scale=lng[:, j:j + 1]).then_inc(s_yg, 1)
                a.wait_ge(s_tv, p + 1)
                a.activation(rstd[:, :], rstd[:, :], ACT.Sqrt).then_inc(s_ts, 1)
                for q in range(2 * TT):
                    n = 16 * p + q
                    a.wait_ge(s_tTps, n + 1)
                    if q >= 2:
                        a.wait_ge(s_gps, n - 1)
                    a.activation(tnT[q % 2], bank[q % 2][:, 0:KC * P].rearrange("p (k m) -> p k m", k=KC),
                                 ACT.Copy).then_inc(s_tT, 1)
            a.wait_ge(s_scat, 16 * TILES)

            def xsT_out(n, u):
                a.wait_ge(s_eTps, n + 1)
                a.activation(xsT[u], bank[0][:, 0:KC * P].rearrange("p (k m) -> p k m", k=KC), ACT.Copy)\
                 .then_inc(s_eT, 1)

            def silu(n, u):
                a.wait_ge(s_h, n + 1)
                a.activation(act1[u], bank[1 + u][:, 0:F], ACT.Silu).then_inc(s_sil, 1)

            xsT_out(0, 0)
            xsT_out(1, 1)
            a.preload_act_table(ACT.Silu)
            with a.Fori(0, NT // 2 - 1) as i:
                for u in range(2):
                    n = i * 2 + u
                    silu(n, u)
                    xsT_out(n + 2, u)
            silu(NT - 2, 0)
            silu(NT - 1, 1)

        @block.vector
        def _(v):
            count = [0]

            def own(ins):
                count[0] += 1
                ins.then_inc(s_vch, 1)
                v.wait_ge(s_vch, count[0])

            v.memset(eps5[:, :], 1e-5)
            v.memset(one[:, :], 1.0).then_inc(s_vset, 1)
            v.sem_inc(s_dbu, C_DBU)
            v.sem_inc(s_scan, C_SCAN)
            v.sem_inc(s_xfree, C_X)
            for p in range(PAIRS):
                for b in range(2):
                    v.wait_ge(s_x[b], 16 * (p + 1))
                    for t in range(TT):
                        ins = v.bn_stats(small[:, b * TT + t, :], xin[b][:, t, :])
                own(ins)
                for t in range(2 * TT):
                    ins = v.bn_aggr(mv[:, t, :], small[:, t, :])
                own(ins)
                v.tensor_scalar(rstd[:, :], mv[:, :, 1], 1e-6, None, ALU.add).then_inc(s_var, 1)
                v.wait_ge(s_std, p + 1)
                own(v.reciprocal(rstd[:, :], rstd[:, :]))
                for b in range(2):
                    for t in range(TT):
                        q = b * TT + t
                        v.tensor_scalar(xin[b][:, t, :], xin[b][:, t, :], mv[:, q, 0:1], rstd[:, q:q + 1],
                                        ALU.subtract, ALU.mult).then_inc(s_xn, 1)
                if p == 0:
                    v.wait_ge(s_const, 16 * (N_CONST - 3))
                    v.tensor_scalar(A, A, MAX_LOG, None, ALU.min).then_inc(s_alog, 1)
                    for k in range(1, ND):
                        own(v.tensor_tensor(dsk[:, 0, :], dsk[:, 0, :], dsk[:, k, :], ALU.add))
                v.wait_ge(s_pad, p + 1)
                for q in range(6):
                    j, h = q // 2, q % 2
                    v.wait_ge(s_proj, p * 12 + q + 1)
                    v.tensor_copy(pad[:, j, 1 + 16 * h:17 + 16 * h, 1:1 + WW],
                                  bank[2 + q].rearrange("p (h w) -> p h w", w=WW)).then_inc(s_xh, 1)
                v.wait_ge(s_xh, p * 6 + 6)
                for t in range(9):
                    dy, dx = t // 3, t % 3
                    for j in range(CG):
                        src = pad[:, j, dy:dy + HH, dx:dx + WW]
                        dst = acc3[:, j, :].rearrange("p (h w) -> p h w", w=WW)
                        if t == 0:
                            ins = v.tensor_scalar(dst, src, cw[:, j, 0:1], cb[:, j:j + 1], ALU.mult, ALU.add)
                        else:
                            ins = v.scalar_tensor_tensor(dst, src, cw[:, j, t:t + 1], dst, ALU.mult, ALU.add)
                        if t == 8:
                            ins.then_inc(s_conv, 1)
                    if t < 8:
                        own(ins)
                lo = slice(64, 128)
                for i, kk in enumerate(PREP):
                    c = ND * p + i
                    par = i % 2
                    hi, mid, low = (t[lo] for t in parts[par])
                    v.wait_ge(s_xd, 2 * c + 2)
                    v.wait_ge(s_hi, 2 * c + 2)
                    if i >= 2:
                        v.wait_ge(s_stack[par], 96 * (2 * p + 1))
                    own(v.tensor_tensor(res[lo], xd[par][lo], hi, ALU.subtract))
                    own(v.tensor_copy(mid, res[lo]))
                    own(v.tensor_tensor(res[lo], res[lo], mid, ALU.subtract))
                    v.tensor_copy(low, res[lo]).then_inc(s_split, 1)
                    v.wait_ge(s_u, c + 1)
                    own(v.scalar_tensor_tensor(one_e, one_e, -1.0, E[par], ALU.add, ALU.subtract))
                    v.wait_ge(s_ln, c + 1)
                    for j in range(CG):
                        ins = v.scalar_tensor_tensor(delta3[par][:, j, :], V3[j], 0.0, delta3[par][:, j, :],
                                                     ALU.max, ALU.add)
                        ins.then_inc(s_vread, 1)
                    v.wait_ge(s_vread, CG * (c + 1))
                    v.tensor_tensor(delta[par], delta[par], one_e, ALU.subtract).then_inc(s_delta, 1)
                v.wait_ge(s_stack[0], 192 * (p + 1))
                v.wait_ge(s_stack[1], 192 * (p + 1))
                for kk in range(ND):
                    c = ND * p + kk
                    if kk < 2:
                        v.wait_ge(s_du, ND * (p + 1))
                    else:
                        v.wait_ge(s_steps[kk - 2], 32 * (p + 1))
                    step = -1 if KORDER[kk] >= 2 else 1

                    with v.Fori(0, NS // U) as i:
                        for u in range(U):
                            n = i * U + u
                            v.wait_ge(s_bc, n * 4 + (c * 4 * NS + 3 + C_BC))
                            v.wait_ge(s_xfree, n + (c * NS + 1 - U + C_X))
                            v.tensor_tensor(X3[u], du3[steps_of(kk)], Bs[u][:, None, :].to_broadcast([P, CG, L]),
                                            ALU.mult).then_inc(s_dbu, 1)
                            v.wait_ge(s_dbu, n + (c * NS + 1 + C_DBU))
                            for j in range(CG):
                                v.wait_ge(s_dA, n * CG + (c * SN + j + 1))
                                v.tensor_tensor_scan(X3[u][:, j, ::step], dA3[u % 2][:, j, ::step],
                                                     X3[u][:, j, ::step], 0.0, ALU.mult, ALU.add)\
                                 .then_inc(s_scan, 1)
                v.wait_ge(s_yrow, CG * (p + 1))
                for j in range(CG):
                    ins = v.scalar_tensor_tensor(y3[:, j, :], xc3[:, j, :], dsk[:, 0, j:j + 1], y3[:, j, :],
                                                 ALU.mult, ALU.add)
                ins.then_inc(s_skip, 1)
                v.wait_ge(s_skip, p + 1)
                v.wait_ge(s_xfree, ND * NS * (p + 1) + C_X)
                for j in range(CG):
                    v.tensor_tensor(y3[:, j, :].rearrange("p (h w) -> p h w", w=WW),
                                    Y3[:, j, :].rearrange("p (w h) -> p h w", w=WW),
                                    y3[:, j, :].rearrange("p (h w) -> p h w", w=WW), ALU.add).then_inc(s_ysum, 1)
                for h in range(2):
                    cs = slice(h * HALF, (h + 1) * HALF)
                    v.wait_ge(s_mean, 2 * p + 2)
                    v.tensor_tensor(y3[:, :, cs], y3[:, :, cs],
                                    bank[h][:, None, :].to_broadcast([P, CG, HALF]), ALU.subtract)\
                     .then_inc(s_yc, 1)
                v.wait_ge(s_std2, 2 * p + 2)
                own(v.reciprocal(std, std))
                v.wait_ge(s_sq, 2 * p + 2)
                for j in range(CG):
                    v.tensor_tensor(y3[:, j, :], y3[:, j, :], std, ALU.mult).then_inc(s_yn, 1)
                for q in range(2 * TT + 1):
                    if q < 2 * TT:
                        if q % TT == 0:
                            v.wait_ge(s_xr[q // TT], 16 * (p + 1))
                        v.wait_ge(s_ops, 16 * p + q + 1)
                        v.tensor_tensor(trow[:, q, 0:DM], bank[4 + q % 4][:, 0:DM], trow[:, q, 0:DM], ALU.add)\
                         .then_inc(s_t, 1)
                    if q:
                        v.wait_ge(s_t, 16 * p + q)
                        ins = v.bn_stats(small[:, q - 1, :], trow[:, q - 1, 0:DM])
                own(ins)
                for t in range(2 * TT):
                    ins = v.bn_aggr(mv[:, t, :], small[:, t, :])
                own(ins)
                v.tensor_scalar(rstd[:, :], mv[:, :, 1], 1e-5, None, ALU.add).then_inc(s_tv, 1)
                v.wait_ge(s_ts, p + 1)
                own(v.reciprocal(rstd[:, :], rstd[:, :]))
                v.tensor_copy(trow[:, :, MEAN], mv[:, :, 0])
                v.tensor_copy(trow[:, :, RSTD], rstd[:, :]).then_inc(s_cols, 1)
                v.wait_ge(s_yz, CG * (p + 1))
                for q in range(2 * TT):
                    if q >= 4:
                        v.wait_ge(s_tTps, 16 * p + q - 3)
                    v.tensor_scalar(tn[q % 4], trow[:, q, 0:DM], mv[:, q, 0:1], rstd[:, q:q + 1],
                                    ALU.subtract, ALU.mult).then_inc(s_tn, 1)
                v.wait_ge(s_gps, 16 * (p + 1))
                v.tensor_tensor(gate[:, p * 2 * TT:(p + 1) * 2 * TT, :],
                                bank[2][:, 0:2 * TT * NE].rearrange("p (t e) -> p t e", e=NE),
                                bg[:, None, :].to_broadcast([P, 2 * TT, NE]), ALU.add).then_inc(s_gate, 1)
            v.wait_ge(s_gate, PAIRS)
            v.wait_ge(s_gch, 4)
            E3 = [P, TILES, NE]
            bc = lambda ap: ap[:, None, :].to_broadcast(E3)
            own(v.tensor_reduce(best, gate[:, :, :], AX_X, ALU.max))
            own(v.tensor_tensor(hot, gate[:, :, :], best[:, :, None].to_broadcast(E3), ALU.is_equal))
            own(v.tensor_tensor(hot, hot, bc(rev), ALU.mult))
            own(v.tensor_reduce(best, hot, AX_X, ALU.max))
            v.tensor_tensor(hot, bc(rev), best[:, :, None].to_broadcast(E3), ALU.is_equal).then_inc(s_hot, 1)
            v.wait_ge(s_cum, 2)
            inside = bank[3][:, 0:TILES * NE].rearrange("p (t e) -> p t e", e=NE)
            totals = bank[4][:, 0:TILES * NE].rearrange("p (t e) -> p t e", e=NE)
            for e in range(NE):
                ins = v.tensor_tensor_scan(pre[:, :, e], ones[:, 0:TILES], totals[:, :, e], 0.0, ALU.mult, ALU.add)
            own(ins)
            own(v.tensor_scalar(cnt, pre[:, TILES - 1, :], float(P - 1), None, ALU.add))
            own(v.tensor_copy(cnt_i, cnt))
            own(v.tensor_scalar(cnt_i, cnt_i, 7, None, ALU.logical_shift_right))
            own(v.tensor_copy(cnt, cnt_i))
            own(v.tensor_tensor_scan(ends, ones[:, 0:NE], cnt, 0.0, ALU.mult, ALU.add))
            own(v.tensor_tensor(base, ends, cnt, ALU.subtract))
            own(v.tensor_scalar(base, base, float(P), None, ALU.mult))
            own(v.tensor_tensor(pre, pre, totals, ALU.subtract))
            own(v.tensor_tensor(pre, pre, inside, ALU.add))
            own(v.tensor_tensor(pre, pre, bc(base), ALU.add))
            own(v.tensor_tensor(pre, pre, hot, ALU.mult))
            own(v.tensor_reduce(slot, pre, AX_X, ALU.add))
            v.tensor_copy(slot_u[:, :], slot).then_inc(s_slot, 1)
            own(v.tensor_tensor(cmp, iota_n[:, :, None].to_broadcast([P, NT, NE]),
                                ends[:, None, :].to_broadcast([P, NT, NE]), ALU.is_ge))
            own(v.tensor_reduce(ef, cmp, AX_X, ALU.add))
            own(v.tensor_scalar(ef, ef, float(NE - 1), None, ALU.min))
            v.tensor_copy(expert_i[:, :], ef).then_inc(s_slot, 1)
            v.wait_ge(s_scat, 16 * TILES)

            def norm(n, k, f):
                v.wait_ge(s_xs[k], f * 16 + 16)
                if not (isinstance(n, int) and n < 2):
                    v.wait_ge(s_eTps, n - 1)
                v.tensor_scalar(xn[k % 2], xs[k][:, 0:DM], xs[k][:, MEAN:MEAN + 1], xs[k][:, RSTD:RSTD + 1],
                                ALU.subtract, ALU.mult).then_inc(s_xnn, 1)

            def gated(n, k):
                u = k % 2
                v.wait_ge(s_sil, n + 1)
                v.tensor_tensor(hid[u], act1[u], bank[3 + u][:, 0:F], ALU.mult).then_inc(s_hid, 1)

            def hidT_out(n, k):
                u = k % 2
                v.wait_ge(s_hTps, n + 1)
                v.tensor_copy(hidT[u][:, 0:FC - 1, :],
                              bank[5][:, 0:(FC - 1) * P].rearrange("p (k m) -> p k m", k=FC - 1)).then_inc(s_hT, 1)
                v.tensor_copy(hidT[u][0:F_LAST, FC - 1, :], bank[5][0:F_LAST, (FC - 1) * P:FC * P])\
                 .then_inc(s_hT, 1)

            def y_out(n, k, stored):
                u = k % 2
                v.wait_ge(s_yps, n + 1)
                if stored is not None:
                    v.wait_ge(s_yst[u], stored * 16)
                v.tensor_tensor(yo[u], bank[6 + u][:, 0:DM], xs[k][:, 0:DM], ALU.add).then_inc(s_yo, 1)

            for n in range(2):
                norm(n, n, 0)
            gated(0, 0)
            for n in (1, 2):
                norm(n + 1, n + 1, 0)
                hidT_out(n - 1, n - 1)
                gated(n, n)
                y_out(n - 1, n - 1, None)
            with v.Fori(0, (NT - 4) // 4) as i:
                for w in range(4):
                    n = i * 4 + (3 + w)
                    norm(n + 1, w, i + 1)
                    hidT_out(n - 1, (2 + w) % 4)
                    gated(n, (3 + w) % 4)
                    y_out(n - 1, (2 + w) % 4, i * 2 + (2 + w) // 2)
            hidT_out(NT - 2, 2)
            gated(NT - 1, 3)
            y_out(NT - 2, 2, (NT - 2) // 2)
            hidT_out(NT - 1, 3)
            y_out(NT - 1, 3, (NT - 1) // 2)

        @block.tensor
        def _(pe):
            pe.wait_ge(s_setup, 1)
            pe.wait_ge(s_vset, 1)
            pe.wait_ge(s_const, 16 * (N_CONST - 3))
            for p in range(PAIRS):
                if p:
                    pe.wait_ge(s_tT, 16 * p)
                for b in range(2):
                    for k in range(KC):
                        for h in range(2):
                            q = (b * KC + k) * 2 + h
                            pe.wait_ge(s_xn, p * 16 + b * TT + 4 * h + 4)
                            if q >= 2:
                                pe.wait_ge(s_xT, p * 12 + q - 1)
                            for t in range(4):
                                ins = pe.transpose(bank[q % 2][:, t * P:(t + 1) * P],
                                                   xin[b][:, h * 4 + t, k * P:(k + 1) * P], ident[:, :])
                            ins.then_inc(s_xTps, 1)
                pe.wait_ge(s_xT, p * 12 + 12)
                pe.wait_ge(s_win, p * 16 + 16)
                if p:
                    pe.wait_ge(s_gate, p)
                for g in range(12):
                    j, h = g // 2, g % 2
                    if g >= 6:
                        pe.wait_ge(s_xh, p * 6 + g - 5)
                    for b in range(2):
                        for k in range(KC):
                            ins = pe.matmul(bank[2 + g % 6][64 * b:64 * b + 64, :],
                                            win[:, k, j * 64:(j + 1) * 64],
                                            xnT[b][:, k, h * HALF:(h + 1) * HALF], start=(k == 0), stop=(k == KC - 1))
                    ins.then_inc(s_proj, 1)
                pe.wait_ge(s_wprep, 32 * (p + 1))
                for i, kk in enumerate(PREP):
                    k = KORDER[kk]
                    c = ND * p + i
                    src = xc3 if kk < 2 else xcT3
                    pe.wait_ge(s_xc, 6 * p + (6 if kk < 2 else 3))
                    if i:
                        pe.wait_ge(s_hi, 2 * c)
                    for h in range(2):
                        for j in range(CG):
                            ins = pe.matmul(bank[h], wxd[:, k, j, :], src[:, j, h * HALF:(h + 1) * HALF],
                                            start=(j == 0), stop=(j == CG - 1))
                        ins.then_inc(s_xdps, 1)
                    if i == 0:
                        pe.wait_ge(s_z, 6 * (p + 1))
                    pe.wait_ge(s_xd, 2 * c + 2)
                    for j in range(CG):
                        if i:
                            pe.wait_ge(s_vread, CG * (c - 1) + j + 1)
                        for h in range(2):
                            ins = pe.matmul(bank[2 + 2 * j + h], wdt[0:64, k, j, :],
                                            xd[i % 2][0:64, h * HALF:(h + 1) * HALF], start=True, stop=True)
                        ins.then_inc(s_vps, 1)

                def spread(kk, n):
                    c = ND * p + kk
                    for h in range(2):
                        for q, st in enumerate((stackB[kk], stackC[kk])):
                            pe.wait_ge(s_bc, n * 4 + (c * 4 * NS + 2 * h + q - 1 + C_BC))
                            lhs = selw[0:96, n, :] if isinstance(n, int) else \
                                selw[0:96, bass.ds(n, 1), :].rearrange("k o m -> k (o m)")
                            pe.matmul(bank[6 + q], lhs, st[0:96, h * HALF:(h + 1) * HALF],
                                      start=True, stop=True).then_inc(s_bcps, 1)

                def sums(kk, n, u, last=False):
                    c = ND * p + kk
                    for j in range(CG):
                        pe.wait_ge(s_hc, n * CG + (c * SN + j + 1 + C_HC))
                        for h in range(2):
                            ins = pe.matmul(Y3[:, j, h * HALF:(h + 1) * HALF], ident[:, :],
                                            X3[u][:, j, h * HALF:(h + 1) * HALF], start=False, stop=last,
                                            skip_group_check=True)
                    ins.then_inc(s_xfree, 1)

                def open_sums():
                    for j in range(CG):
                        for h in range(2):
                            pe.matmul(Y3[:, j, h * HALF:(h + 1) * HALF], zero_mm[0:96, :],
                                      selw[0:96, 0:HALF // P, :].rearrange("k n m -> k (n m)"),
                                      start=True, stop=False, skip_group_check=True)

                pe.wait_ge(s_vread, CG * ND * (p + 1))
                pe.wait_ge(s_hi, 2 * ND * (p + 1))
                pe.wait_ge(s_stack[0], 192 * (p + 1))
                pe.wait_ge(s_stack[1], 192 * (p + 1))
                open_sums()
                spread(0, 0)
                spread(0, 1)
                for kk in range(ND):
                    if kk == 2:
                        pe.wait_ge(s_yrow, CG * (p + 1))
                        open_sums()
                    with pe.Fori(0, NS // U - 1) as i:
                        for u in range(U):
                            spread(kk, i * U + u + 2)
                            sums(kk, i * U + u, u)
                    for u in range(U):
                        n = NS - U + u
                        if n + 2 < NS:
                            spread(kk, n + 2)
                        elif n + 2 == NS and kk + 1 < ND:
                            spread(kk + 1, 0)
                        sums(kk, n, u, last=(kk % 2 == 1 and u == U - 1))
                    if kk + 1 < ND:
                        spread(kk + 1, 1)
                pe.wait_ge(s_ysum, CG * (p + 1))
                for h in range(2):
                    for j in range(CG):
                        ins = pe.matmul(bank[h], mean_w[:, :], y3[:, j, h * HALF:(h + 1) * HALF],
                                        start=(j == 0), stop=(j == CG - 1))
                    ins.then_inc(s_mean, 1)
                for h in range(2):
                    pe.wait_ge(s_sq, 2 * p + h + 1)
                    for j in range(CG):
                        ins = pe.matmul(bank[2 + h], mean_w[:, :], sq3[:, j, h * HALF:(h + 1) * HALF],
                                        start=(j == 0), stop=(j == CG - 1))
                    ins.then_inc(s_var2, 1)
                pe.wait_ge(s_yz, CG * (p + 1))
                for q in range(2 * TT):
                    b, t = q // TT, q % TT
                    if q >= 4:
                        pe.wait_ge(s_t, p * 16 + q - 3)
                    for j in range(CG):
                        ins = pe.matmul(bank[4 + q % 4][:, 0:DM], y3[64 * b:64 * b + 64, j, t * P:(t + 1) * P],
                                        wout[64 * b:64 * b + 64, j, :], start=(j == 0), stop=(j == CG - 1))
                    ins.then_inc(s_ops, 1)
                for q in range(2 * TT + 1):
                    if q < 2 * TT:
                        pe.wait_ge(s_tn, 16 * p + q + 1)
                        if q >= 2:
                            pe.wait_ge(s_tT, 16 * p + q - 1)
                        for k in range(KC):
                            ins = pe.transpose(bank[q % 2][:, k * P:(k + 1) * P], tn[q % 4][:, k * P:(k + 1) * P],
                                               ident[:, :])
                        ins.then_inc(s_tTps, 1)
                    if q >= 1:
                        n = q - 1
                        pe.wait_ge(s_tT, 16 * p + n + 1)
                        for k in range(KC):
                            ins = pe.matmul(bank[2][:, n * NE:(n + 1) * NE], tnT[n % 2][:, k, :], wg[:, k, :],
                                            start=(k == 0), stop=(k == KC - 1))
                        ins.then_inc(s_gps, 1)
            pe.wait_ge(s_hot, 1)
            hotf = hot.rearrange("p t e -> p (t e)")
            pe.matmul(bank[3][:, 0:TILES * NE], tri[:, :], hotf, start=True, stop=True).then_inc(s_cum, 1)
            pe.matmul(bank[4][:, 0:TILES * NE], ones[:, :], hotf, start=True, stop=True).then_inc(s_cum, 1)
            pe.wait_ge(s_slot, 2)
            pe.wait_ge(s_scat, 16 * TILES)
            pe.wait_ge(s_wl, 16 * (2 * KC + FC))
            expert_reg = [pe.alloc_register("expert_even"), pe.alloc_register("expert_odd")]

            def fetch_expert(n, u):
                at = expert_i[0:1, n:n + 1] if isinstance(n, int) else expert_i[0:1, bass.ds(n, 1)]
                pe.reg_load(expert_reg[u], at)

            def expert(u):
                return pe.snap(expert_reg[u], min_val=0, max_val=NE - 1)

            def rows_T(n, u):
                pe.wait_ge(s_xnn, n + 1)
                if not (isinstance(n, int) and n == 0):
                    pe.wait_ge(s_eT, n)
                for k in range(KC):
                    ins = pe.transpose(bank[0][:, k * P:(k + 1) * P], xn[u][:, k * P:(k + 1) * P], ident[:, :])
                ins.then_inc(s_eTps, 1)

            def hidden(n, u, e):
                pe.wait_ge(s_eT, n + 1)
                if not (isinstance(n, int) and n < 2):
                    pe.wait_ge(s_hid, n - 1)
                for w, bk in ((W1, bank[1 + u]), (W2, bank[3 + u])):
                    for k in range(KC):
                        ins = pe.matmul(bk[:, 0:F], xsT[u][:, k, :], w[:, k, bass.ds(e * F, F)],
                                        start=(k == 0), stop=(k == KC - 1))
                ins.then_inc(s_h, 1)

            def hidden_T(n, u):
                pe.wait_ge(s_hid, n + 1)
                if not (isinstance(n, int) and n == 0):
                    pe.wait_ge(s_hT, n * 2)
                for k in range(FC):
                    m = P if k < FC - 1 else F_LAST
                    ins = pe.transpose(bank[5][0:m, k * P:(k + 1) * P], hid[u][:, k * P:k * P + m], ident[:, :])
                ins.then_inc(s_hTps, 1)

            def down(n, u, e):
                pe.wait_ge(s_hT, n * 2 + 2)
                if not (isinstance(n, int) and n < 2):
                    pe.wait_ge(s_yo, n - 1)
                for k in range(FC):
                    m = P if k < FC - 1 else F_LAST
                    ins = pe.matmul(bank[6 + u][:, 0:DM], hidT[u][0:m, k, :], W3[0:m, k, bass.ds(e * DM, DM)],
                                    start=(k == 0), stop=(k == FC - 1))
                ins.then_inc(s_yps, 1)

            def tile_step(n, u, more=True):
                e, e_before = expert(u), expert(1 - u)
                hidden(n, u, e)
                if more:
                    fetch_expert(n + 1, 1 - u)
                hidden_T(n - 1, 1 - u)
                if more:
                    rows_T(n + 1, 1 - u)
                down(n - 1, 1 - u, e_before)

            fetch_expert(0, 0)
            rows_T(0, 0)
            rows_T(1, 1)
            hidden(0, 0, expert(0))
            fetch_expert(1, 1)
            tile_step(1, 1)
            tile_step(2, 0)
            with pe.Fori(0, (NT - 4) // 2) as i:
                tile_step(i * 2 + 3, 1)
                tile_step(i * 2 + 4, 0)
            tile_step(NT - 1, 1, more=False)
            hidden_T(NT - 1, 1)
            down(NT - 1, 1, expert(1))


def kernel(**inputs):
    import ml_dtypes
    import numpy as np
    import concourse.bacc as _bacc
    from concourse.bass_utils import run_bass_kernel_spmd as _run

    a = {k.replace("L0_", ""): np.asarray(v) for k, v in inputs.items()}
    f4 = np.float32

    def both(v):
        v = v.reshape((CG, 64) + v.shape[1:])
        v = np.moveaxis(v, 1, 0)
        return np.ascontiguousarray(np.concatenate([v, v], axis=0))

    w_in = np.ascontiguousarray(a["conv_in_proj_w"].T.reshape(KC, P, 2 * DI).transpose(1, 0, 2))
    xp = a["conv_x_proj_w"]
    w_xd = np.zeros((P, ND, CG, P), f4)
    w_dt = np.zeros((64, ND, CG, P), f4)
    for k in range(ND):
        for j in range(CG):
            for b in range(2):
                rows = slice(64 * b, 64 * b + 64)
                ch = slice(64 * j, 64 * j + 64)
                w_xd[rows, k, j, 32 * b:32 * b + R] = xp[k, 0:R, ch].T
                w_xd[rows, k, j, 64 + 16 * b:80 + 16 * b] = xp[k, R:R + NS, ch].T
                w_xd[rows, k, j, 96 + 16 * b:112 + 16 * b] = xp[k, R + NS:, ch].T
                w_dt[32 * b:32 * b + R, k, j, rows] = a["conv_dt_projs_w"][k, ch, :].T
                w_dt[32 * b + R, k, j, rows] = a["conv_dt_projs_b"][k, ch]
    bias_row = np.zeros((P, 1), f4)
    bias_row[[R, 32 + R]] = 1
    sel = np.zeros((96, NS, P), ml_dtypes.bfloat16)
    for q in range(96):
        b, n = (q // 16) % 2, q % 16
        sel[q, n, 64 * b:64 * b + 64] = 1
    half_ones = np.zeros((P, P), f4)
    half_ones[0:64, 0:64] = 1.0 / DI
    half_ones[64:, 64:] = 1.0 / DI
    w3 = np.zeros((FC * P, NE * DM), f4)
    w3[0:F] = a["ffn_W3"].transpose(2, 0, 1).reshape(F, NE * DM)
    arrays = dict(
        x=np.ascontiguousarray(a["x"].reshape(NB, L, DM)),
        w_in=w_in,
        conv_w=both(a["conv_conv_w"].reshape(DI, 9)),
        conv_b=both(a["conv_conv_b"]),
        w_xd=w_xd, w_dt=w_dt,
        bias_row=bias_row,
        a_log=np.ascontiguousarray(both(a["conv_A_logs"].reshape(ND, DI, NS).transpose(1, 0, 2)).transpose(0, 2, 1, 3)),
        d_skip=np.ascontiguousarray(both(a["conv_Ds"].reshape(ND, DI).T).transpose(0, 2, 1)),
        ln_g=both(a["conv_out_norm_g"]), ln_b=both(a["conv_out_norm_b"]),
        w_out=both(np.ascontiguousarray(a["conv_out_proj_w"].T)),
        w_gate=np.ascontiguousarray(a["ffn_Wg"].T.reshape(KC, P, NE).transpose(1, 0, 2)),
        b_gate=np.ascontiguousarray(a["ffn_bg"]),
        w1=np.ascontiguousarray(a["ffn_W1"].transpose(2, 0, 1).reshape(KC, P, NE * F)),
        w2=np.ascontiguousarray(a["ffn_W2"].transpose(2, 0, 1).reshape(KC, P, NE * F)),
        w3=w3.reshape(FC, P, NE * DM),
        sel=sel, ident_d=np.eye(P, dtype=f4), half_ones=half_ones,
        tri_d=np.triu(np.ones((P, P), f4), 1),
    )
    nc = _bacc.Bacc("TRN2", target_bir_lowering=False, num_devices=1)
    feed, aps = {}, {}
    for name, v in arrays.items():
        feed["in_" + name] = v
        aps[name] = nc.dram_tensor("in_" + name, v.shape, mybir.dt.from_np(v.dtype), kind="ExternalInput").ap()
    out = nc.dram_tensor("out_0", (TOK, DM), F32, kind="ExternalOutput").ap()
    build(nc, **aps, out=out)
    r = _run(nc, [feed], core_ids=[0])
    return r.results[0]["out_0"].reshape(NB, HH, WW, DM)
```

```python
from contextlib import ExitStack

import concourse.bass as bass
from concourse import mybir

F32 = mybir.dt.float32
BF16 = mybir.dt.bfloat16
I32 = mybir.dt.int32
U32 = mybir.dt.uint32
ALU = mybir.AluOpType
ACT = mybir.ActivationFunctionType
AX_X = mybir.AxisListType.X

P = 128
NB, HH, WW, DM = 4, 32, 32, 384
L = HH * WW
DI, NS, R, ND = 192, 16, 24, 4
PAIRS = NB // 2
CG = 3
KC = DM // P
TT = L // P
HALF = 512
NE, F = 8, 469
FC = 4
TOK = NB * L
TILES = TOK // P
NT = TILES + NE
PW = WW + 2
U = 4
KORDER = (0, 2, 1, 3)
PREP = (2, 3, 0, 1)
ROW = DM + 2
MEAN, RSTD = DM, DM + 1
MAX_LOG = 80.5
F_LAST = F - (FC - 1) * P


def build(nc, x, w_in, conv_w, conv_b, w_xd, w_dt, bias_row, a_log, d_skip, ln_g, ln_b, w_out,
          w_gate, b_gate, w1, w2, w3, sel, ident_d, half_ones, tri_d, out):
    ctx = ExitStack()
    with ctx:
        def sb(name, shape, dt=F32):
            return ctx.enter_context(nc.sbuf_tensor(name, shape, dt))

        def sem(name):
            return ctx.enter_context(nc.semaphore(name))

        def sems(*ns):
            return [sem(n) for n in ns]

        z_dram = nc.dram_tensor("z_dram", [P, CG * L], F32, kind="Internal").ap()
        step_dram = nc.dram_tensor("step_dram", [2, 2, P, CG * L], F32, kind="Internal").ap()
        t_dram = nc.dram_tensor("t_dram", [TOK, ROW], F32, kind="Internal").ap()

        ident = sb("ident", [P, P])
        ones = sb("ones", [P, P])
        mean_w = sb("mean_w", [P, P])
        tri = sb("tri", [P, P])
        eps5 = sb("eps5", [P, 1])
        one = sb("one", [P, 1])
        small_in = sb("small_in", [P, 16, 6])
        mv_in = sb("mv_in", [P, 16, 2])
        rstd_in = sb("rstd_in", [P, 16])
        small = sb("small", [P, 16, 6])
        mv = sb("mv", [P, 16, 2])
        rstd = sb("rstd", [P, 16])
        gate = sb("gate", [P, TILES, NE])
        wg = sb("wg", [P, KC, NE])
        bg = sb("bg", [P, NE])
        lane = sb("lane", [P, 1])
        expert_i = sb("expert_i", [P, NT], I32)

        ARENA = 51400
        arena = sb("arena", [P, ARENA])
        top = [0]

        def carve(n):
            at = top[0]
            top[0] += n
            assert top[0] <= ARENA, top[0]
            return arena[:, at:at + n]

        GL = CG * L
        g3 = lambda ap: ap.rearrange("p (j l) -> p j l", j=CG)
        X = [carve(GL) for _ in range(U)]
        dA = [carve(GL) for _ in range(2)]
        delta, du = [None] * 2, [None] * 2
        for i in range(2):
            delta[i], du[i] = carve(GL), carve(GL)
        Bs = [carve(L) for _ in range(U)]
        post_at = top[0]
        Cs = [carve(L) for _ in range(U)]
        stackB = [carve(L // 2).bitcast(BF16) for _ in range(ND)]
        stackC = [carve(L // 2).bitcast(BF16) for _ in range(ND)]
        y = carve(GL)
        xc_at = top[0]
        xc = carve(GL)
        late_at = top[0]
        selw = carve(NS * P // 2).bitcast(BF16).rearrange("p (n m) -> p n m", n=NS)
        A = carve(ND * CG * NS).rearrange("p (k j n) -> p k j n", k=ND, j=CG)
        wout = carve(2 * DM).rearrange("p (c m) -> p c m", c=2)
        cw = carve(CG * 9).rearrange("p (j t) -> p j t", j=CG)
        cb = carve(CG)
        brow = carve(1)
        dsk = carve(ND * CG).rearrange("p (k j) -> p k j", k=ND)
        lng = carve(CG)
        lnb = carve(CG)
        zero_mm = carve(P // 2).bitcast(BF16)
        X3, dA3, delta3, du3 = ([g3(t) for t in ts_] for ts_ in (X, dA, delta, du))
        xc3, y3 = g3(xc), g3(y)
        xin = [X[b].rearrange("p (t c) -> p t c", t=TT) for b in range(2)]
        xnT = [dA[b].rearrange("p (k l) -> p k l", k=KC) for b in range(2)]
        padf = arena[:, 2 * GL:2 * GL + CG * PW * PW]
        pad = padf.rearrange("p (j h w) -> p j h w", j=CG, h=PW)
        acc3 = delta3[0]
        taps_at = 2 * GL + CG * PW * PW
        tap = [arena[:, taps_at + i * L:taps_at + (i + 1) * L] for i in range(2)]
        win = du[0][:, 0:KC * DM].rearrange("p (k m) -> p k m", k=KC)
        zs = arena[:, 10 * GL:11 * GL]
        zs3 = g3(zs)
        xcT, xcT3 = X[0], X3[0]
        E = [X[1], X[2]]
        one_e = X[3]
        ln_e = arena[:, post_at:post_at + GL]
        xd = [dA[0][:, 0:L], dA[0][:, L:2 * L]]
        res = dA[0][:, 2 * L:3 * L]
        parts = [[dA[1][:, (3 * i + r) * (L // 2):(3 * i + r + 1) * (L // 2)].bitcast(BF16) for r in range(3)]
                 for i in range(2)]
        wxd = y[:, 0:CG * ND * P].rearrange("p (k j m) -> p k j m", k=ND, j=CG)
        wdt = y[:, CG * ND * P:2 * CG * ND * P].rearrange("p (k j m) -> p k j m", k=ND, j=CG)
        top[0] = post_at
        trow = carve(2 * TT * ROW).rearrange("p (t c) -> p t c", t=2 * TT)
        row_of = trow.rearrange("p (t b) c -> p t b c", b=2)
        sq = du[1]
        sq3 = g3(sq)
        yz3 = sq3
        std = carve(L)
        route_at = top[0]
        z2 = xc
        tn = [arena[:, xc_at + i * DM:xc_at + (i + 1) * DM] for i in range(4)]
        tnT = [arena[:, xc_at + (4 + i) * DM:xc_at + (5 + i) * DM].rearrange("p (k m) -> p k m", k=KC)
               for i in range(2)]
        top[0] = 0
        W1 = carve(KC * NE * F).rearrange("p (k n) -> p k n", k=KC)
        W2 = carve(KC * NE * F).rearrange("p (k n) -> p k n", k=KC)
        W3 = carve(FC * NE * DM).rearrange("p (k n) -> p k n", k=FC)
        assert top[0] <= post_at
        top[0] = route_at
        in_place = carve(TILES * P // 2).bitcast(BF16).rearrange("p (t m) -> p t m", t=TILES)
        in_tile = carve(TILES * NT // 2).bitcast(BF16).rearrange("p (t n) -> p t n", t=TILES)
        number_of = carve(TILES * NT).bitcast(BF16).rearrange("p (t w n) -> p t w n", t=TILES, w=2)
        assert top[0] <= xc_at
        top[0] = late_at
        iota_n = carve(NT)
        rev = carve(NE)
        hot = carve(TILES * NE).rearrange("p (t e) -> p t e", t=TILES)
        pre = carve(TILES * NE).rearrange("p (t e) -> p t e", t=TILES)
        best = carve(TILES)
        cnt = carve(NE)
        cnt_i = carve(NE).bitcast(I32)
        ends = carve(NE)
        base = carve(NE)
        slot = carve(TILES)
        cmp = carve(NE * NT).rearrange("p (n e) -> p n e", e=NE)
        ef = carve(NT)
        iota_m = carve(P)
        block_no = carve(TILES)
        slot_i = carve(TILES).bitcast(I32)
        tile_f = carve(TILES)
        place_f = carve(TILES)
        parts_f = carve(2 * NT)
        number1 = carve(NT)
        is_pad = carve(NT)
        moves = carve(2 * NT).rearrange("p (n w) -> p n w", w=2)
        top[0] = post_at
        xs = [carve(ROW) for _ in range(4)]
        xn = [carve(DM) for _ in range(2)]
        xsT = [carve(KC * P).rearrange("p (k m) -> p k m", k=KC) for _ in range(2)]
        act1 = [carve(F) for _ in range(2)]
        hid = [carve(F) for _ in range(2)]
        hidT = [carve(FC * P).rearrange("p (k m) -> p k m", k=FC) for _ in range(2)]
        yo = [carve(DM) for _ in range(2)]
        first_rows = sb("first_rows", [P, 4], U32)
        move = sb("move", [P, 4, 2], U32)
        gap = sb("gap", [P, 4])

        psum = ctx.enter_context(nc.psum_tensor("psum", [P, 8, HALF], F32))
        bank = [psum[:, i, :] for i in range(8)]
        Y3 = psum[:, 0:6, :].rearrange("p (j h) n -> p j (h n)", j=CG)
        V3 = [psum[:, 2 + 2 * j:4 + 2 * j, :].rearrange("p h n -> p (h n)") for j in range(CG)]

        s_const, s_setup, s_vset, s_alog = sems("const_loaded", "setup_done", "dve_setup", "a_log_clamped")
        s_x = sems("x_loaded_0", "x_loaded_1")
        s_var, s_std, s_xn, s_xTps, s_xT, s_win, s_proj, s_xh, s_z, s_zst, s_pad, s_conv, s_xc, s_xcr = sems(
            "var_ready", "std_ready", "xn_ready", "xT_in_psum", "xT_ready", "win_loaded", "proj_in_psum",
            "xh_ready", "z_ready", "z_stored", "pad_cleared", "conv_done", "xc_columns_ready",
            "xc_rows_ready")
        (s_wprep, s_xdps, s_xd, s_hi, s_split, s_vps, s_abs, s_e, s_ln, s_u, s_vread, s_relu, s_delta,
         s_delta_v, s_du) = sems(
            "prep_weights", "xd_in_psum", "xd_ready", "hi_ready", "split_ready", "dt_in_psum", "abs_ready",
            "exp_ready", "ln_ready", "one_plus_e_ready", "dt_read", "relu_ready", "delta_of_pool_ready",
            "delta_of_dve_ready", "du_ready")
        s_stack = sems("stack_loaded_0", "stack_loaded_1")
        s_dst = sems("delta_stored_0", "delta_stored_1")
        s_dust = sems("du_stored_0", "du_stored_1")
        s_steps = sems("step_loaded_0", "step_loaded_1")
        s_bcps, s_bc, s_dA, s_dbu, s_scan, s_hc, s_xfree = sems(
            "bc_in_psum", "bc_ready", "dA_ready", "dbu_ready", "scan_done", "hc_ready", "x_slot_free")
        s_yrow, s_skip, s_ysum, s_mean, s_yc, s_sq, s_var2, s_std2, s_yn, s_yg, s_zld, s_yz, s_yzp = sems(
            "y_row_taken", "skip_added", "y_summed", "mean_in_psum", "yc_ready", "sq_ready", "var_in_psum",
            "std2_ready", "yn_ready", "yg_ready", "z_loaded", "yz_ready", "yz_of_pool_ready")
        s_xr = sems("x_again_0", "x_again_1")
        s_ops, s_t, s_tv, s_ts, s_cols, s_tn, s_tTps, s_tT, s_gps, s_gate, s_tst = sems(
            "out_in_psum", "t_ready", "t_var_ready", "t_std_ready", "row_columns", "tn_ready",
            "tnT_in_psum", "tnT_ready", "gate_in_psum", "gate_ready", "t_stored")
        s_prod, s_taps, s_vch, s_ach, s_iota = sems(
            "tap_product", "taps_summed", "dve_chain", "act_chain", "iotas_ready")
        s_wl, s_hot, s_cum, s_slot, s_tile, s_num, s_sorted, s_first = sems(
            "expert_weights", "hot_ready", "counts_in_psum", "slots_ready", "tile_of_token", "numbers_ready",
            "order_in_psum", "first_rows_ready")
        s_xs = [sem(f"xs_loaded_{i}") for i in range(4)]
        s_yst = sems("y_tile_stored_0", "y_tile_stored_1")
        s_gap, s_xnn, s_eTps, s_eT, s_h, s_sil, s_hid, s_hTps, s_hT, s_yps, s_yo = sems(
            "gap_written", "tile_normed", "xsT_in_psum", "xsT_ready", "hidden_in_psum", "silu_ready", "hidden_ready",
            "hiddenT_in_psum", "hiddenT_ready", "y_tile_in_psum", "y_tile_ready")

        C_BC, C_DBU, C_SCAN, C_HC, C_X = 2, U, 2 * CG, U, U
        N_CONST = 14
        BY_POOL = CG - 1
        ORDER = (0, BY_POOL, 1)
        GROUPS = 2 * TT // 4
        SN = CG * NS
        steps_of = lambda kk: kk % 2

        block = ctx.enter_context(nc.Block())

        @block.sync
        def _(sp):
            def load_x(p):
                for b in range(2):
                    sp.dma_start(xin[b], x[2 * p + b].rearrange("(t q) c -> q t c", q=P)).then_inc(s_x[b], 16)
                sp.dma_start(win, w_in).then_inc(s_win, 16)

            sp.dma_start(xin[0], x[0].rearrange("(t q) c -> q t c", q=P)).then_inc(s_x[0], 16)
            sp.dma_start(ident[:, :], ident_d).then_inc(s_const, 16)
            sp.dma_start(xin[1], x[1].rearrange("(t q) c -> q t c", q=P)).then_inc(s_x[1], 16)
            sp.dma_start(win, w_in).then_inc(s_win, 16)
            for dst, src in ((mean_w[:, :], half_ones), (tri[:, :], tri_d), (selw[0:96], sel), (A, a_log),
                             (cw, conv_w), (cb, conv_b), (brow, bias_row), (dsk, d_skip), (lng, ln_g),
                             (lnb, ln_b), (wout, w_out), (wg[:, :, :], w_gate),
                             (bg[:, :], b_gate.partition_broadcast(P))):
                sp.dma_start(dst, src).then_inc(s_const, 16)

            for p in range(PAIRS):
                if p:
                    sp.wait_ge(s_ops, 16 * p)
                sp.dma_start(wxd, w_xd).then_inc(s_wprep, 16)
                sp.dma_start(wdt[0:64], w_dt).then_inc(s_wprep, 16)
                sp.wait_ge(s_z, 6 * (p + 1))
                if p:
                    sp.wait_ge(s_zld, 16 * p)
                    sp.wait_ge(s_tst, 16 * 2 * GROUPS)
                sp.dma_start(z_dram, zs).then_inc(s_zst, 16)

                def store_steps(i):
                    sp.wait_ge(s_delta, CG * ((ND - 1) * p + i + 1))
                    sp.dma_start(step_dram[i, 0], delta[i]).then_inc(s_dst[i], 16)
                    sp.wait_ge(s_du, CG * (ND * p + i + 1))
                    sp.dma_start(step_dram[i, 1], du[i]).then_inc(s_dust[i], 16)

                for i, kk in enumerate(PREP):
                    sp.wait_ge(s_split, ND * p + i + 1)
                    for r, part in enumerate(parts[i % 2]):
                        sp.dma_start(stackB[kk][32 * r:32 * r + 32, :], part[64:96, :]).then_inc(s_stack[i % 2], 16)
                        sp.dma_start(stackC[kk][32 * r:32 * r + 32, :], part[96:128, :]).then_inc(s_stack[i % 2], 16)
                    if i in (1, 2):
                        store_steps(i - 1)
                for i in range(2):
                    sp.wait_ge(s_scan, (ND * p + i + 1) * SN + C_SCAN)
                    sp.wait_ge(s_dst[i], 16 * (p + 1))
                    sp.wait_ge(s_dust[i], 16 * (p + 1))
                    sp.dma_start(delta[i], step_dram[i, 0]).then_inc(s_steps[i], 16)
                    sp.dma_start(du[i], step_dram[i, 1]).then_inc(s_steps[i], 16)
                if p + 1 < PAIRS:
                    sp.wait_ge(s_xfree, ND * NS * (p + 1) - 2 + C_X)
                    load_x(p + 1)
                sp.wait_ge(s_xfree, ND * NS * (p + 1) + C_X)

                def x_again(b):
                    sp.dma_start(row_of[:, :, b, 0:DM],
                                 x[2 * p + b].rearrange("(t q) c -> q t c", q=P)).then_inc(s_xr[b], 16)

                x_again(0)
                x_again(1)
                sp.wait_ge(s_skip, p + 1)
                sp.wait_ge(s_zst, 16 * (p + 1))
                sp.dma_start(z2, z_dram).then_inc(s_zld, 16)
                if p + 1 == PAIRS:
                    sp.wait_ge(s_var2, 2 * PAIRS)
                    for k in range(KC):
                        sp.dma_start(W1[:, k, :], w1[k]).then_inc(s_wl, 16)
                for g in range(GROUPS):
                    sp.wait_ge(s_cols, GROUPS * p + g + 1)
                    for b in range(2):
                        at = (2 * p + b) * L + 2 * g * P
                        sp.dma_start(t_dram[at:at + 2 * P, :].rearrange("(t q) c -> q t c", q=P),
                                     row_of[:, 2 * g:2 * g + 2, b, :]).then_inc(s_tst, 16)
                    if p + 1 == PAIRS and g < KC:
                        sp.dma_start(W2[:, g, :], w2[g]).then_inc(s_wl, 16)
            sp.wait_ge(s_ops, 16 * PAIRS)
            for k in range(FC):
                sp.dma_start(W3[:, k, :], w3[k]).then_inc(s_wl, 16)
            sp.wait_ge(s_wl, 16 * (2 * KC + FC))

        @block.gpsimd
        def _(g):
            g.memset(padf, 0.0).then_inc(s_pad, 1)
            g.memset(ones[:, :], 1.0)
            g.memset(zero_mm, 0.0).then_inc(s_setup, 1)
            g.sem_inc(s_hc, C_HC)
            g.sem_inc(s_gap, 4)
            g.iota(lane[:, :], [[0, 1]], base=1, channel_multiplier=1, allow_small_or_imprecise_dtypes=True)\
             .then_inc(s_iota, 1)
            for p in range(PAIRS):
                if p:
                    g.memset(padf, 0.0).then_inc(s_pad, 1)
                for t in range(1, 9):
                    g.wait_ge(s_prod, 9 * p + t + 1)
                    if t > 1:
                        g.wait_ge(s_taps, 8 * p + t - 1)
                    g.tensor_tensor(acc3[:, BY_POOL, :], acc3[:, BY_POOL, :], tap[t % 2], ALU.add).then_inc(s_taps, 1)
                for i, kk in enumerate(PREP):
                    if i >= 2:
                        g.wait_ge(s_dust[i % 2], 16 * (p + 1))
                    for j in range(CG):
                        n, d = CG * (ND * p + i) + j + 1, delta3[i % 2][:, j, :]
                        if i < ND - 1:
                            done = CG * ((ND - 1) * p + i) + j + 1
                            g.wait_ge(s_relu, n)
                            g.wait_ge(s_ln, n)
                            g.tensor_tensor(d, d, g3(ln_e)[:, j, :], ALU.add).then_inc(s_delta, 1)
                            g.wait_ge(s_delta, done)
                        else:
                            g.wait_ge(s_delta_v, CG * p + j + 1)
                        g.tensor_tensor(du3[i % 2][:, j, :], d, (xc3 if kk < 2 else xcT3)[:, j, :], ALU.mult)\
                         .then_inc(s_du, 1)
                for kk in range(ND):
                    c = ND * p + kk
                    with g.Fori(0, NS // U) as i:
                        for u in range(U):
                            n = i * U + u
                            g.wait_ge(s_bc, n * 4 + (c * 4 * NS + 4 + C_BC))
                            g.wait_ge(s_scan, n * CG + (c * SN + CG + C_SCAN))
                            g.tensor_tensor(X3[u], X3[u], Cs[u][:, None, :].to_broadcast([P, CG, L]), ALU.mult)\
                             .then_inc(s_hc, 1)
                g.wait_ge(s_zld, 16 * (p + 1))
                for h in range(2):
                    cs = slice(h * HALF, (h + 1) * HALF)
                    g.wait_ge(s_yg, 2 * CG * p + CG * h + 1)
                    for b in range(2):
                        src = slice(64 * b, 64 * b + 64)
                        ins = g.tensor_tensor(yz3[0:64, b, cs], y3[src, 0, cs], g3(z2)[src, 0, cs], ALU.mult)
                    ins.then_inc(s_yzp, 1)
            g.wait_ge(s_ops, 16 * PAIRS)
            small_ok = dict(allow_small_or_imprecise_dtypes=True)
            g.iota(iota_n, [[1, NT]], base=0, channel_multiplier=0, **small_ok).then_inc(s_iota, 1)
            g.iota(rev, [[-1, NE]], base=NE, channel_multiplier=0, **small_ok).then_inc(s_iota, 1)
            g.iota(iota_m, [[1, P]], base=0, channel_multiplier=0, **small_ok).then_inc(s_iota, 1)
            g.iota(block_no, [[2 * TT, PAIRS], [1, TT], [TT, 2]], base=0, channel_multiplier=0, **small_ok)\
             .then_inc(s_iota, 1)
            g.wait_ge(s_iota, 5)
            g.wait_ge(s_tile, 1)
            g.tensor_tensor(number_of[:, :, 0, :], in_tile, block_no[:, :, None].to_broadcast([P, TILES, NT]),
                            ALU.mult).then_inc(s_num, 1)
            g.wait_ge(s_tst, 16 * 2 * GROUPS * PAIRS)
            g.wait_ge(s_first, 1)

            def load_rows(k, rows):
                g.indirect_dma_start(xs[k], None, t_dram, bass.IndirectOffsetOnAxis(rows, 0)).then_inc(s_xs[k], 16)

            for k in range(4):
                load_rows(k, first_rows[:, k:k + 1])

            def store_rows(n, k, more):
                g.wait_ge(s_gap, n + 1)
                g.wait_ge(s_yo, n + 1)
                g.tensor_tensor(gap[:, k:k + 1], one[:, :], one[:, :], ALU.mult).then_inc(s_gap, 1)
                g.indirect_dma_start(out, bass.IndirectOffsetOnAxis(move[:, k, 0:1], 0), yo[k % 2], None,
                                     bounds_check=TOK - 1, oob_is_err=False).then_inc(s_yst[k % 2], 16)
                if more:
                    load_rows(k, move[:, k, 1:2])

            with g.Fori(0, NT // 4 - 1) as i:
                for w in range(4):
                    store_rows(i * 4 + w, w, True)
            for w in range(4):
                store_rows(NT - 4 + w, w, False)
            for u in range(2):
                g.wait_ge(s_yst[u], 16 * (NT // 2))

        @block.scalar
        def _(a):
            count = [0]

            def own(ins):
                count[0] += 1
                ins.then_inc(s_ach, 1)
                a.wait_ge(s_ach, count[0])

            def norm_std(p, b):
                cols = slice(b * TT, (b + 1) * TT)
                a.wait_ge(s_var, 2 * p + b + 1)
                a.activation(rstd_in[:, cols], rstd_in[:, cols], ACT.Sqrt).then_inc(s_std, 1)

            a.sem_inc(s_bc, C_BC)
            for p in range(PAIRS):
                if p == 0:
                    for b in range(2):
                        norm_std(0, b)
                for b in range(2):
                    for k in range(KC):
                        for h in range(2):
                            q = (b * KC + k) * 2 + h
                            a.wait_ge(s_xTps, p * 12 + q + 1)
                            a.activation(xnT[b][:, k, h * HALF:(h + 1) * HALF], bank[q % 2], ACT.Copy)\
                             .then_inc(s_xT, 1)
                def xh_out(q):
                    j, h = ORDER[q // 2], q % 2
                    a.wait_ge(s_proj, p * 12 + q + 1)
                    a.activation(pad[:, j, 1 + 16 * h:17 + 16 * h, 1:1 + WW],
                                 bank[2 + q].rearrange("p (h w) -> p h w", w=WW), ACT.Copy).then_inc(s_xh, 1)

                def z_out(q):
                    a.wait_ge(s_proj, p * 12 + 6 + q + 1)
                    j, h = q // 2, q % 2
                    a.activation(zs3[:, j, h * HALF:(h + 1) * HALF], bank[2 + q], ACT.Silu).then_inc(s_z, 1)

                def product(t):
                    src = pad[:, BY_POOL, t // 3:t // 3 + HH, t % 3:t % 3 + WW]
                    if t == 0:
                        a.wait_ge(s_xh, p * 6 + 4)
                        a.activation(acc3[:, BY_POOL, :].rearrange("p (h w) -> p h w", w=WW), src, ACT.Identity,
                                     bias=cb[:, BY_POOL:BY_POOL + 1], scale=cw[:, BY_POOL, 0:1]).then_inc(s_prod, 1)
                        return
                    if t >= 3:
                        a.wait_ge(s_taps, 8 * p + t - 2)
                    a.activation(tap[t % 2].rearrange("p (h w) -> p h w", w=WW), src, ACT.Copy,
                                 scale=cw[:, BY_POOL, t:t + 1]).then_inc(s_prod, 1)

                a.wait_ge(s_pad, p + 1)
                if p == 0:
                    a.wait_ge(s_const, 16 * N_CONST)
                for q in range(4):
                    xh_out(q)
                product(0)
                product(1)
                product(2)
                xh_out(4)
                xh_out(5)
                product(3)
                for q in range(5):
                    z_out(q)
                    product(4 + q)
                z_out(5)
                if p:
                    a.wait_ge(s_gps, 16 * p)
                for j in ORDER:
                    if j == BY_POOL:
                        a.wait_ge(s_taps, 8 * (p + 1))
                    else:
                        a.wait_ge(s_conv, p * (CG - 1) + j + 1)
                    a.activation(xcT3[:, j, :].rearrange("p (w h) -> p w h", w=WW),
                                 acc3[:, j, :].rearrange("p (h w) -> p w h", w=WW), ACT.Silu).then_inc(s_xc, 1)
                    if j != ORDER[-1]:
                        a.activation(xc3[:, j, :], acc3[:, j, :], ACT.Silu).then_inc(s_xcr, 1)
                j = ORDER[-1]
                a.activation(xc3[:, j, :], acc3[:, j, :], ACT.Silu).then_inc(s_xcr, 1)
                a.preload_act_table_set("natural_log_exp_and_others")
                if p == 0:
                    a.wait_ge(s_alog, 1)
                    own(a.activation(A, A, ACT.Exp))
                    own(a.mul(A, A, -1.0))
                def xd_out(i):
                    c, par = ND * p + i, i % 2
                    if i >= 2:
                        a.wait_ge(s_vps, 3 * (c - 1))
                        a.wait_ge(s_split, c - 1)
                        a.wait_ge(s_stack[par], 96 * (2 * p + 1))
                    for h in range(2):
                        cs = slice(h * HALF, (h + 1) * HALF)
                        a.wait_ge(s_xdps, 2 * c + h + 1)
                        a.activation(xd[par][:, cs], bank[h], ACT.Identity, bias=brow).then_inc(s_xd, 1)
                        a.activation(parts[par][0][64:128, cs], bank[h][64:128, :], ACT.Copy).then_inc(s_hi, 1)

                xd_out(0)
                if p:
                    a.wait_ge(s_tst, 16 * 2 * GROUPS)
                for i in range(ND):
                    c, par = ND * p + i, i % 2
                    E3 = g3(E[par])
                    if i >= 2:
                        a.wait_ge(s_relu, CG * (c - 1))
                    for j in range(CG):
                        a.wait_ge(s_vps, CG * c + j + 1)
                        a.activation(E3[:, j, :], V3[j], ACT.Abs).then_inc(s_abs, 1)
                    if 0 < i < ND - 1:
                        xd_out(i + 1)
                    for j in range(CG):
                        a.wait_ge(s_abs, CG * c + j + 1)
                        a.activation(E3[:, j, :], E3[:, j, :], ACT.Exp, scale=-1.0).then_inc(s_e, 1)
                    if i == 0:
                        xd_out(1)
                    for j in range(CG):
                        n = CG * c + j + 1
                        a.wait_ge(s_e, n)
                        if i:
                            a.wait_ge(s_relu, n - CG)
                            a.wait_ge(s_delta, CG * ((ND - 1) * p + i - 1) + j + 1)
                        a.activation(g3(one_e)[:, j, :], E3[:, j, :], ACT.Identity, bias=one[:, :]).then_inc(s_u, 1)
                        a.activation(g3(ln_e)[:, j, :], E3[:, j, :], ACT.Ln, bias=one[:, :]).then_inc(s_ln, 1)

                def copies(kk, n, u):
                    c = ND * p + kk
                    a.wait_ge(s_dbu, n + (c * NS + 1 - U + C_DBU))
                    a.wait_ge(s_hc, n + (c * NS + 1 - U + C_HC))
                    for h in range(2):
                        for q, dst in enumerate((Bs[u], Cs[u])):
                            a.wait_ge(s_bcps, n * 4 + (c * 4 * NS + 2 * h + q + 1))
                            a.activation(dst[:, h * HALF:(h + 1) * HALF], bank[6 + q], ACT.Copy).then_inc(s_bc, 1)

                def exps(kk, n, u):
                    c = ND * p + kk
                    for j in range(CG):
                        a.wait_ge(s_scan, n * CG + (c * SN + j + 1 - 2 * CG + C_SCAN))
                        a.activation(dA3[u % 2][:, j, :], delta3[steps_of(kk)][:, j, :], ACT.Exp,
                                     scale=A[:, KORDER[kk], j, n:n + 1] if isinstance(n, int)
                                     else A[:, KORDER[kk], j, bass.ds(n, 1)]).then_inc(s_dA, 1)

                a.wait_ge(s_zst, 16 * (p + 1))
                a.wait_ge(s_delta, CG * (ND - 1) * (p + 1))
                a.wait_ge(s_delta_v, CG * (p + 1))
                a.wait_ge(s_stack[0], 192 * (p + 1))
                a.wait_ge(s_stack[1], 192 * (p + 1))
                copies(0, 0, 0)
                for kk in range(ND):
                    if kk >= 2:
                        a.wait_ge(s_steps[kk - 2], 32 * (p + 1))
                    for u in range(U):
                        exps(kk, u, u)
                        copies(kk, u + 1, (u + 1) % U)
                        if kk == 2 and u == 2:
                            a.wait_ge(s_xfree, (ND * p + 2) * NS + C_X)
                            for j in range(CG):
                                a.activation(y3[:, j, :], Y3[:, j, :], ACT.Copy).then_inc(s_yrow, 1)
                    with a.Fori(1, NS // U - 1) as i:
                        for u in range(U):
                            exps(kk, i * U + u, u)
                            copies(kk, i * U + u + 1, (u + 1) % U)
                    for u in range(U):
                        n = NS - U + u
                        exps(kk, n, u)
                        if n + 1 < NS:
                            copies(kk, n + 1, (u + 1) % U)
                        elif kk + 1 < ND:
                            copies(kk + 1, 0, 0)
                for h in range(2):
                    cs = slice(h * HALF, (h + 1) * HALF)
                    a.wait_ge(s_yc, 2 * p + h + 1)
                    a.activation(sq3[:, :, cs], y3[:, :, cs], ACT.Square).then_inc(s_sq, 1)
                for h in range(2):
                    a.wait_ge(s_var2, 2 * p + h + 1)
                    a.activation(std[:, h * HALF:(h + 1) * HALF], bank[2 + h], ACT.Sqrt, bias=eps5[:, :])\
                     .then_inc(s_std2, 1)
                if p + 1 < PAIRS:
                    for b in range(2):
                        norm_std(p + 1, b)
                for h in range(2):
                    cs = slice(h * HALF, (h + 1) * HALF)
                    a.wait_ge(s_yn, 2 * p + h + 1)
                    for j in range(CG):
                        a.activation(y3[:, j, cs], y3[:, j, cs], ACT.Identity, bias=lnb[:, j:j + 1],
                                     scale=lng[:, j:j + 1]).then_inc(s_yg, 1)
                for g in range(GROUPS + 1):
                    if g:
                        for q in range(4 * g - 4, 4 * g):
                            n = 16 * p + q
                            a.wait_ge(s_tTps, n + 1)
                            if q >= 2:
                                a.wait_ge(s_gps, n - 1)
                            a.activation(tnT[q % 2], bank[q % 2][:, 0:KC * P].rearrange("p (k m) -> p k m", k=KC),
                                         ACT.Copy).then_inc(s_tT, 1)
                    if g < GROUPS:
                        a.wait_ge(s_tv, GROUPS * p + g + 1)
                        a.activation(rstd[:, 4 * g:4 * g + 4], rstd[:, 4 * g:4 * g + 4], ACT.Sqrt).then_inc(s_ts, 1)

            def xsT_out(n, u):
                a.wait_ge(s_eTps, n + 1)
                a.activation(xsT[u], bank[0][:, 0:KC * P].rearrange("p (k m) -> p k m", k=KC), ACT.Copy)\
                 .then_inc(s_eT, 1)

            def silu(n, u):
                a.wait_ge(s_h, n * 2 + 1)
                a.activation(act1[u], bank[1 + u][:, 0:F], ACT.Silu).then_inc(s_sil, 1)

            xsT_out(0, 0)
            xsT_out(1, 1)
            a.preload_act_table(ACT.Silu)
            with a.Fori(0, NT // 2 - 1) as i:
                for u in range(2):
                    n = i * 2 + u
                    silu(n, u)
                    xsT_out(n + 2, u)
            silu(NT - 2, 0)
            silu(NT - 1, 1)

        @block.vector
        def _(v):
            count = [0]

            def own(ins):
                count[0] += 1
                ins.then_inc(s_vch, 1)
                v.wait_ge(s_vch, count[0])

            v.memset(eps5[:, :], 1e-5)
            v.memset(one[:, :], 1.0).then_inc(s_vset, 1)
            v.sem_inc(s_dbu, C_DBU)
            v.sem_inc(s_scan, C_SCAN)
            v.sem_inc(s_xfree, C_X)
            def norm_stats(p, b):
                rows = range(b * TT, (b + 1) * TT)
                v.wait_ge(s_x[b], 16 * (p + 1))
                for q in rows:
                    ins = v.bn_stats(small_in[:, q, :], xin[b][:, q - b * TT, :])
                own(ins)
                for q in rows:
                    ins = v.bn_aggr(mv_in[:, q, :], small_in[:, q, :])
                own(ins)
                v.tensor_scalar(rstd_in[:, b * TT:(b + 1) * TT], mv_in[:, b * TT:(b + 1) * TT, 1], 1e-6, None,
                                ALU.add).then_inc(s_var, 1)

            def norm_rows(p, b):
                cols = slice(b * TT, (b + 1) * TT)
                v.wait_ge(s_std, 2 * p + b + 1)
                own(v.reciprocal(rstd_in[:, cols], rstd_in[:, cols]))
                for t in range(TT):
                    q = b * TT + t
                    v.tensor_scalar(xin[b][:, t, :], xin[b][:, t, :], mv_in[:, q, 0:1], rstd_in[:, q:q + 1],
                                    ALU.subtract, ALU.mult).then_inc(s_xn, 1)

            for p in range(PAIRS):
                if p == 0:
                    for b in range(2):
                        norm_stats(0, b)
                        norm_rows(0, b)
                if p == 0:
                    v.wait_ge(s_const, 16 * N_CONST)
                    v.tensor_scalar(A, A, MAX_LOG, None, ALU.min).then_inc(s_alog, 1)
                    for k in range(1, ND):
                        own(v.tensor_tensor(dsk[:, 0, :], dsk[:, 0, :], dsk[:, k, :], ALU.add))
                for j in range(CG - 1):
                    v.wait_ge(s_xh, p * 6 + (2 if j == 0 else 6))
                    dst = acc3[:, j, :].rearrange("p (h w) -> p h w", w=WW)
                    for t in range(9):
                        src = pad[:, j, t // 3:t // 3 + HH, t % 3:t % 3 + WW]
                        if t == 0:
                            own(v.tensor_scalar(dst, src, cw[:, j, 0:1], cb[:, j:j + 1], ALU.mult, ALU.add))
                        else:
                            ins = v.scalar_tensor_tensor(dst, src, cw[:, j, t:t + 1], dst, ALU.mult, ALU.add)
                            if t < 8:
                                own(ins)
                    ins.then_inc(s_conv, 1)
                lo = slice(64, 128)

                def split(i):
                    c, par = ND * p + i, i % 2
                    hi, mid, low = (t[lo] for t in parts[par])
                    v.wait_ge(s_xd, 2 * c + 2)
                    v.wait_ge(s_hi, 2 * c + 2)
                    if i >= 2:
                        v.wait_ge(s_stack[par], 96 * (2 * p + 1))
                    if c:
                        v.wait_ge(s_split, c)
                    own(v.tensor_tensor(res[lo], xd[par][lo], hi, ALU.subtract))
                    own(v.tensor_copy(mid, res[lo]))
                    own(v.tensor_tensor(res[lo], res[lo], mid, ALU.subtract))
                    v.tensor_copy(low, res[lo]).then_inc(s_split, 1)

                split(0)
                v.wait_ge(s_xcr, CG * (p + 1))
                for i in range(ND):
                    c, par = ND * p + i, i % 2
                    if i >= 2:
                        v.wait_ge(s_dst[par], 16 * (p + 1))
                    for j in range(CG):
                        v.wait_ge(s_abs, CG * c + j + 1)
                        if i >= 2:
                            v.wait_ge(s_du, CG * (c - 2) + j + 1)
                        v.tensor_scalar(delta3[par][:, j, :], V3[j], 0.0, None, ALU.max).then_inc(s_vread, 1)
                    if i + 1 < ND:
                        split(i + 1)
                    for j in range(CG):
                        v.wait_ge(s_u, CG * c + j + 1)
                        u3, e3 = g3(one_e)[:, j, :], g3(E[par])[:, j, :]
                        own(v.scalar_tensor_tensor(u3, u3, -1.0, e3, ALU.add, ALU.subtract))
                        d = delta3[par][:, j, :]
                        v.tensor_tensor(d, d, u3, ALU.subtract).then_inc(s_relu, 1)
                        if i == ND - 1:
                            v.wait_ge(s_relu, CG * c + j + 1)
                            v.wait_ge(s_ln, CG * c + j + 1)
                            v.tensor_tensor(d, d, g3(ln_e)[:, j, :], ALU.add).then_inc(s_delta_v, 1)
                v.wait_ge(s_ln, CG * ND * (p + 1))
                v.wait_ge(s_relu, CG * ND * (p + 1))
                v.wait_ge(s_stack[0], 192 * (p + 1))
                v.wait_ge(s_stack[1], 192 * (p + 1))
                def input_of(kk, n, u):
                    c = ND * p + kk
                    v.wait_ge(s_bc, n * 4 + (c * 4 * NS + 3 + C_BC))
                    v.wait_ge(s_xfree, n + (c * NS + 1 - U + C_X))
                    v.tensor_tensor(X3[u], du3[steps_of(kk)], Bs[u][:, None, :].to_broadcast([P, CG, L]),
                                    ALU.mult).then_inc(s_dbu, 1)

                def scans(kk, n, u):
                    c, step = ND * p + kk, -1 if KORDER[kk] >= 2 else 1
                    v.wait_ge(s_dbu, n + (c * NS + 1 + C_DBU))
                    for j in range(CG):
                        v.wait_ge(s_dA, n * CG + (c * SN + j + 1))
                        v.tensor_tensor_scan(X3[u][:, j, ::step], dA3[u % 2][:, j, ::step],
                                             X3[u][:, j, ::step], 0.0, ALU.mult, ALU.add).then_inc(s_scan, 1)

                def steps_ready(kk):
                    if kk < 2:
                        v.wait_ge(s_du, CG * (ND * p + 3 + kk))
                    else:
                        v.wait_ge(s_steps[kk - 2], 32 * (p + 1))

                steps_ready(0)
                input_of(0, 0, 0)
                for kk in range(ND):
                    with v.Fori(0, NS // U - 1) as i:
                        for u in range(U):
                            input_of(kk, i * U + (u + 1), (u + 1) % U)
                            scans(kk, i * U + u, u)
                    for u in range(U):
                        n = NS - U + u
                        if n + 1 < NS:
                            input_of(kk, n + 1, u + 1)
                        elif kk + 1 < ND:
                            steps_ready(kk + 1)
                            input_of(kk + 1, 0, 0)
                        scans(kk, n, u)
                v.wait_ge(s_yrow, CG * (p + 1))
                for j in range(CG):
                    ins = v.scalar_tensor_tensor(y3[:, j, :], xc3[:, j, :], dsk[:, 0, j:j + 1], y3[:, j, :],
                                                 ALU.mult, ALU.add)
                ins.then_inc(s_skip, 1)
                if p + 1 < PAIRS:
                    norm_stats(p + 1, 0)
                v.wait_ge(s_skip, p + 1)
                v.wait_ge(s_xfree, ND * NS * (p + 1) + C_X)
                for j in range(CG):
                    v.tensor_tensor(y3[:, j, :].rearrange("p (h w) -> p h w", w=WW),
                                    Y3[:, j, :].rearrange("p (w h) -> p h w", w=WW),
                                    y3[:, j, :].rearrange("p (h w) -> p h w", w=WW), ALU.add).then_inc(s_ysum, 1)
                if p + 1 < PAIRS:
                    norm_stats(p + 1, 1)
                for h in range(2):
                    cs = slice(h * HALF, (h + 1) * HALF)
                    v.wait_ge(s_mean, 2 * p + h + 1)
                    v.tensor_tensor(y3[:, :, cs], y3[:, :, cs],
                                    bank[h][:, None, :].to_broadcast([P, CG, HALF]), ALU.subtract)\
                     .then_inc(s_yc, 1)
                def scale(h):
                    cs = slice(h * HALF, (h + 1) * HALF)
                    v.wait_ge(s_std2, 2 * p + h + 1)
                    own(v.reciprocal(std[:, cs], std[:, cs]))
                    v.wait_ge(s_sq, 2 * p + h + 1)
                    v.tensor_tensor(y3[:, :, cs], y3[:, :, cs], std[:, None, cs].to_broadcast([P, CG, HALF]),
                                    ALU.mult).then_inc(s_yn, 1)

                def times_z(h):
                    cs = slice(h * HALF, (h + 1) * HALF)
                    v.wait_ge(s_yg, 2 * CG * p + CG * h + 2)
                    for b in range(2):
                        src = slice(64 * b, 64 * b + 64)
                        v.tensor_tensor(yz3[64:128, b, cs], y3[src, 1, cs], g3(z2)[src, 1, cs], ALU.mult)
                    v.wait_ge(s_yg, 2 * CG * p + CG * h + 3)
                    v.tensor_tensor(yz3[:, 2, cs], y3[:, 2, cs], g3(z2)[:, 2, cs], ALU.mult).then_inc(s_yz, 1)

                scale(0)
                scale(1)
                v.wait_ge(s_zld, 16 * (p + 1))
                times_z(0)
                times_z(1)
                for b in range(2):
                    v.wait_ge(s_xr[b], 16 * (p + 1))
                v.wait_ge(s_yz, 2 * (p + 1))
                v.wait_ge(s_yzp, 2 * (p + 1))
                for g in range(GROUPS):
                    rows, cols = range(4 * g, 4 * g + 4), slice(4 * g, 4 * g + 4)
                    for q in rows:
                        v.wait_ge(s_ops, 16 * p + q + 1)
                        v.tensor_tensor(trow[:, q, 0:DM], bank[4 + q % 4][:, 0:DM], trow[:, q, 0:DM], ALU.add)\
                         .then_inc(s_t, 1)
                    for q in rows:
                        v.wait_ge(s_t, 16 * p + q + 1)
                        ins = v.bn_stats(small[:, q, :], trow[:, q, 0:DM])
                    own(ins)
                    for q in rows:
                        ins = v.bn_aggr(mv[:, q, :], small[:, q, :])
                    own(ins)
                    v.tensor_scalar(rstd[:, cols], mv[:, cols, 1], 1e-5, None, ALU.add).then_inc(s_tv, 1)
                    v.wait_ge(s_ts, GROUPS * p + g + 1)
                    own(v.reciprocal(rstd[:, cols], rstd[:, cols]))
                    for q in rows:
                        if q >= 4:
                            v.wait_ge(s_tTps, 16 * p + q - 3)
                        v.tensor_scalar(tn[q % 4], trow[:, q, 0:DM], mv[:, q, 0:1], rstd[:, q:q + 1],
                                        ALU.subtract, ALU.mult).then_inc(s_tn, 1)
                    v.tensor_copy(trow[:, cols, MEAN], mv[:, cols, 0])
                    v.tensor_copy(trow[:, cols, RSTD], rstd[:, cols]).then_inc(s_cols, 1)
                    if p + 1 < PAIRS:
                        if g in (1, 2):
                            norm_rows(p + 1, g - 1)
                v.wait_ge(s_gps, 16 * (p + 1))
                v.tensor_tensor(gate[:, p * 2 * TT:(p + 1) * 2 * TT, :],
                                bank[2][:, 0:2 * TT * NE].rearrange("p (t e) -> p t e", e=NE),
                                bg[:, None, :].to_broadcast([P, 2 * TT, NE]), ALU.add).then_inc(s_gate, 1)
            v.wait_ge(s_gate, PAIRS)
            v.wait_ge(s_iota, 5)
            E3 = [P, TILES, NE]
            bc = lambda ap: ap[:, None, :].to_broadcast(E3)
            own(v.tensor_reduce(best, gate[:, :, :], AX_X, ALU.max))
            own(v.tensor_tensor(hot, gate[:, :, :], best[:, :, None].to_broadcast(E3), ALU.is_equal))
            own(v.tensor_tensor(hot, hot, bc(rev), ALU.mult))
            own(v.tensor_reduce(best, hot, AX_X, ALU.max))
            v.tensor_tensor(hot, bc(rev), best[:, :, None].to_broadcast(E3), ALU.is_equal).then_inc(s_hot, 1)
            v.wait_ge(s_cum, 2)
            inside = bank[3][:, 0:TILES * NE].rearrange("p (t e) -> p t e", e=NE)
            totals = bank[4][:, 0:TILES * NE].rearrange("p (t e) -> p t e", e=NE)
            for e in range(NE):
                ins = v.tensor_tensor_scan(pre[:, :, e], ones[:, 0:TILES], totals[:, :, e], 0.0, ALU.mult, ALU.add)
            own(ins)
            own(v.tensor_scalar(cnt, pre[:, TILES - 1, :], float(P - 1), None, ALU.add))
            own(v.tensor_copy(cnt_i, cnt))
            own(v.tensor_scalar(cnt_i, cnt_i, 7, None, ALU.logical_shift_right))
            own(v.tensor_copy(cnt, cnt_i))
            own(v.tensor_tensor_scan(ends, ones[:, 0:NE], cnt, 0.0, ALU.mult, ALU.add))
            own(v.tensor_tensor(base, ends, cnt, ALU.subtract))
            own(v.tensor_scalar(base, base, float(P), None, ALU.mult))
            own(v.tensor_tensor(pre, pre, totals, ALU.subtract))
            own(v.tensor_tensor(pre, pre, inside, ALU.add))
            own(v.tensor_tensor(pre, pre, bc(base), ALU.add))
            own(v.tensor_tensor(pre, pre, hot, ALU.mult))
            own(v.tensor_reduce(slot, pre, AX_X, ALU.add))
            own(v.tensor_copy(slot_i, slot))
            own(v.tensor_scalar(slot_i, slot_i, 7, None, ALU.logical_shift_right))
            own(v.tensor_copy(tile_f, slot_i))
            own(v.scalar_tensor_tensor(place_f, tile_f, float(-P), slot, ALU.mult, ALU.add))
            v.tensor_tensor(in_tile, iota_n[:, None, :].to_broadcast([P, TILES, NT]),
                            tile_f[:, :, None].to_broadcast([P, TILES, NT]), ALU.is_equal).then_inc(s_tile, 1)
            v.tensor_tensor(in_place, iota_m[:, None, :].to_broadcast([P, TILES, P]),
                            place_f[:, :, None].to_broadcast([P, TILES, P]), ALU.is_equal).then_inc(s_num, 1)
            v.wait_ge(s_tile, 1)
            v.tensor_scalar(number_of[:, :, 1, :], in_tile, lane[:, :], None, ALU.mult).then_inc(s_num, 1)
            own(v.tensor_tensor(cmp, iota_n[:, :, None].to_broadcast([P, NT, NE]),
                                ends[:, None, :].to_broadcast([P, NT, NE]), ALU.is_ge))
            own(v.tensor_reduce(ef, cmp, AX_X, ALU.add))
            own(v.tensor_scalar(ef, ef, float(NE - 1), None, ALU.min))
            v.tensor_copy(expert_i[:, :], ef).then_inc(s_slot, 1)
            v.wait_ge(s_sorted, 1)
            own(v.tensor_copy(parts_f, bank[5][:, 0:2 * NT]))
            own(v.scalar_tensor_tensor(number1, parts_f[:, 0:NT], float(P), parts_f[:, NT:2 * NT],
                                       ALU.mult, ALU.add))
            v.tensor_scalar(first_rows[:, :], number1[:, 0:4], -1.0, 0.0, ALU.add, ALU.max).then_inc(s_first, 1)
            own(v.tensor_scalar(is_pad, number1, 0.0, float(TOK + 1), ALU.is_equal, ALU.mult))
            v.memset(moves[:, NT - 4:NT, 1], 0.0)
            v.tensor_scalar(moves[:, 0:NT - 4, 1], number1[:, 4:NT], -1.0, 0.0, ALU.add, ALU.max)
            own(v.scalar_tensor_tensor(moves[:, :, 0], number1, -1.0, is_pad, ALU.add, ALU.add))
            def norm(n, k, f):
                v.wait_ge(s_xs[k], f * 16 + 16)
                if not (isinstance(n, int) and n < 2):
                    v.wait_ge(s_eTps, n - 1)
                v.tensor_scalar(xn[k % 2], xs[k][:, 0:DM], xs[k][:, MEAN:MEAN + 1], xs[k][:, RSTD:RSTD + 1],
                                ALU.subtract, ALU.mult).then_inc(s_xnn, 1)

            def gated(n, k):
                u = k % 2
                v.wait_ge(s_sil, n + 1)
                v.wait_ge(s_h, n * 2 + 2)
                v.tensor_tensor(hid[u], act1[u], bank[3 + u][:, 0:F], ALU.mult).then_inc(s_hid, 1)

            def hidT_out(n, k):
                u = k % 2
                v.wait_ge(s_hTps, n + 1)
                v.tensor_copy(hidT[u][:, 0:FC - 1, :],
                              bank[5][:, 0:(FC - 1) * P].rearrange("p (k m) -> p k m", k=FC - 1)).then_inc(s_hT, 1)
                v.tensor_copy(hidT[u][0:F_LAST, FC - 1, :], bank[5][0:F_LAST, (FC - 1) * P:FC * P])\
                 .then_inc(s_hT, 1)

            def y_out(n, k, stored):
                u = k % 2
                v.wait_ge(s_yps, n + 1)
                if stored is not None:
                    v.wait_ge(s_yst[u], stored * 16)
                at = slice(n, n + 1) if isinstance(n, int) else bass.ds(n, 1)
                v.tensor_scalar(move[:, k:k + 1, :], moves[:, at, :], 0.0, None, ALU.add)
                v.tensor_tensor(yo[u], bank[6 + u][:, 0:DM], xs[k][:, 0:DM], ALU.add).then_inc(s_yo, 1)

            for n in range(2):
                norm(n, n, 0)
            gated(0, 0)
            for n in (1, 2):
                norm(n + 1, n + 1, 0)
                hidT_out(n - 1, n - 1)
                gated(n, n)
                y_out(n - 1, n - 1, None)
            with v.Fori(0, (NT - 4) // 4) as i:
                for w in range(4):
                    n = i * 4 + (3 + w)
                    norm(n + 1, w, i + 1)
                    hidT_out(n - 1, (2 + w) % 4)
                    gated(n, (3 + w) % 4)
                    y_out(n - 1, (2 + w) % 4, i * 2 + (2 + w) // 2)
            hidT_out(NT - 2, 2)
            gated(NT - 1, 3)
            y_out(NT - 2, 2, (NT - 2) // 2)
            hidT_out(NT - 1, 3)
            y_out(NT - 1, 3, (NT - 1) // 2)

        @block.tensor
        def _(pe):
            pe.wait_ge(s_setup, 1)
            pe.wait_ge(s_vset, 1)
            pe.wait_ge(s_const, 16 * N_CONST)
            for p in range(PAIRS):
                if p:
                    pe.wait_ge(s_tT, 16 * p)
                for b in range(2):
                    for k in range(KC):
                        for h in range(2):
                            q = (b * KC + k) * 2 + h
                            pe.wait_ge(s_xn, p * 16 + b * TT + 4 * h + 4)
                            if q >= 2:
                                pe.wait_ge(s_xT, p * 12 + q - 1)
                            for t in range(4):
                                ins = pe.transpose(bank[q % 2][:, t * P:(t + 1) * P],
                                                   xin[b][:, h * 4 + t, k * P:(k + 1) * P], ident[:, :])
                            ins.then_inc(s_xTps, 1)
                pe.wait_ge(s_xT, p * 12 + 12)
                pe.wait_ge(s_win, p * 16 + 16)
                if p:
                    pe.wait_ge(s_gate, p)
                for g in range(12):
                    j, h = g // 2, g % 2
                    if j < CG:
                        j = ORDER[j]
                    if g >= 6:
                        pe.wait_ge(s_xh, p * 6 + g - 5)
                    for k in range(KC):
                        for b in range(2):
                            ins = pe.matmul(bank[2 + g % 6][64 * b:64 * b + 64, :],
                                            win[:, k, j * 64:(j + 1) * 64],
                                            xnT[b][:, k, h * HALF:(h + 1) * HALF], start=(k == 0), stop=(k == KC - 1))
                    ins.then_inc(s_proj, 1)
                pe.wait_ge(s_wprep, 32 * (p + 1))
                def xd_rows(i):
                    kk, c = PREP[i], ND * p + i
                    src = xc3 if kk < 2 else xcT3
                    if i:
                        pe.wait_ge(s_hi, 2 * c)
                    for h in range(2):
                        for w, j in enumerate(ORDER):
                            if h == 0:
                                pe.wait_ge(s_xcr if kk < 2 else s_xc, CG * p + w + 1)
                            ins = pe.matmul(bank[h], wxd[:, KORDER[kk], j, :], src[:, j, h * HALF:(h + 1) * HALF],
                                            start=(w == 0), stop=(w == CG - 1))
                        ins.then_inc(s_xdps, 1)

                xd_rows(0)
                pe.wait_ge(s_z, 6 * (p + 1))
                for i in range(ND):
                    c = ND * p + i
                    if 0 < i < ND - 1:
                        xd_rows(i + 1)
                    pe.wait_ge(s_xd, 2 * c + 2)
                    for j in range(CG):
                        if i:
                            pe.wait_ge(s_vread, CG * (c - 1) + j + 1)
                        for h in range(2):
                            ins = pe.matmul(bank[2 + 2 * j + h], wdt[0:64, KORDER[PREP[i]], j, :],
                                            xd[i % 2][0:64, h * HALF:(h + 1) * HALF], start=True, stop=True)
                        ins.then_inc(s_vps, 1)
                    if i == 0:
                        xd_rows(1)

                def spread(kk, n, halves=(0, 1)):
                    c = ND * p + kk
                    for h in halves:
                        for q, st in enumerate((stackB[kk], stackC[kk])):
                            pe.wait_ge(s_bc, n * 4 + (c * 4 * NS + 2 * h + q - 1 + C_BC))
                            lhs = selw[0:96, n, :] if isinstance(n, int) else \
                                selw[0:96, bass.ds(n, 1), :].rearrange("k o m -> k (o m)")
                            pe.matmul(bank[6 + q], lhs, st[0:96, h * HALF:(h + 1) * HALF],
                                      start=True, stop=True).then_inc(s_bcps, 1)

                def step(kk, n, u, then, last=False):
                    pe.wait_ge(s_hc, n + ((ND * p + kk) * NS + 1 + C_HC))
                    if then:
                        spread(*then, halves=(0,))
                    for j in range(CG):
                        if then and j == 1:
                            spread(*then, halves=(1,))
                        for h in range(2):
                            ins = pe.matmul(Y3[:, j, h * HALF:(h + 1) * HALF], ident[:, :],
                                            X3[u][:, j, h * HALF:(h + 1) * HALF], start=False, stop=last,
                                            skip_group_check=True)
                    ins.then_inc(s_xfree, 1)

                def open_sums():
                    for j in range(CG):
                        for h in range(2):
                            pe.matmul(Y3[:, j, h * HALF:(h + 1) * HALF], zero_mm[0:96, :],
                                      selw[0:96, 0:HALF // P, :].rearrange("k n m -> k (n m)"),
                                      start=True, stop=False, skip_group_check=True)

                pe.wait_ge(s_vread, CG * ND * (p + 1))
                pe.wait_ge(s_hi, 2 * ND * (p + 1))
                pe.wait_ge(s_stack[0], 192 * (p + 1))
                pe.wait_ge(s_stack[1], 192 * (p + 1))
                open_sums()
                for n in range(U):
                    spread(0, n)
                for kk in range(ND):
                    if kk == 2:
                        pe.wait_ge(s_yrow, CG * (p + 1))
                        open_sums()
                    with pe.Fori(0, NS // U - 1) as i:
                        for u in range(U):
                            step(kk, i * U + u, u, (kk, i * U + (u + U)))
                    for u in range(U):
                        n = NS - U + u
                        then = (kk, n + U) if n + U < NS else (kk + 1, n + U - NS) if kk + 1 < ND else None
                        step(kk, n, u, then, last=(kk % 2 == 1 and u == U - 1))
                pe.wait_ge(s_ysum, CG * (p + 1))
                for h in range(2):
                    for j in range(CG):
                        ins = pe.matmul(bank[h], mean_w[:, :], y3[:, j, h * HALF:(h + 1) * HALF],
                                        start=(j == 0), stop=(j == CG - 1))
                    ins.then_inc(s_mean, 1)
                for h in range(2):
                    pe.wait_ge(s_sq, 2 * p + h + 1)
                    for j in range(CG):
                        ins = pe.matmul(bank[2 + h], mean_w[:, :], sq3[:, j, h * HALF:(h + 1) * HALF],
                                        start=(j == 0), stop=(j == CG - 1))
                    ins.then_inc(s_var2, 1)
                def project(q):
                    for w in range(2):
                        if q >= 4:
                            pe.wait_ge(s_t, p * 16 + q + w - 3)
                    tokens = slice(q // 2 * P, (q // 2 + 1) * P)
                    for b in range(2):
                        pe.matmul(bank[4 + (q + b) % 4][:, 0:DM], yz3[:, b, tokens], wout[:, 0, :],
                                  start=True, stop=False)
                    for b in range(2):
                        half = slice(64 * b, 64 * b + 64)
                        pe.matmul(bank[4 + (q + b) % 4][:, 0:DM], yz3[half, 2, tokens], wout[half, 1, :],
                                  start=False, stop=True).then_inc(s_ops, 1)

                def rows_to_channels(q):
                    pe.wait_ge(s_tn, 16 * p + q + 1)
                    if q >= 2:
                        pe.wait_ge(s_tT, 16 * p + q - 1)
                    for k in range(KC):
                        ins = pe.transpose(bank[q % 2][:, k * P:(k + 1) * P], tn[q % 4][:, k * P:(k + 1) * P],
                                           ident[:, :])
                    ins.then_inc(s_tTps, 1)

                def gates(q):
                    pe.wait_ge(s_tT, 16 * p + q + 1)
                    for k in range(KC):
                        ins = pe.matmul(bank[2][:, q * NE:(q + 1) * NE], tnT[q % 2][:, k, :], wg[:, k, :],
                                        start=(k == 0), stop=(k == KC - 1))
                    ins.then_inc(s_gps, 1)

                for g in range(GROUPS + 1):
                    if g < GROUPS:
                        pe.wait_ge(s_yz, 2 * p + g // 2 + 1)
                        pe.wait_ge(s_yzp, 2 * p + g // 2 + 1)
                        project(4 * g)
                        project(4 * g + 2)
                    if g:
                        for q in range(4 * g - 4, 4 * g):
                            rows_to_channels(q)
                            if q:
                                gates(q - 1)
                gates(2 * TT - 1)
            pe.wait_ge(s_hot, 1)
            hotf = hot.rearrange("p t e -> p (t e)")
            pe.matmul(bank[3][:, 0:TILES * NE], tri[:, :], hotf, start=True, stop=True).then_inc(s_cum, 1)
            pe.matmul(bank[4][:, 0:TILES * NE], ones[:, :], hotf, start=True, stop=True).then_inc(s_cum, 1)
            pe.wait_ge(s_num, 3)
            for t in range(TILES):
                ins = pe.matmul(bank[5][:, 0:2 * NT], in_place[:, t, :],
                                number_of[:, t, :, :].rearrange("p w n -> p (w n)"),
                                start=(t == 0), stop=(t == TILES - 1))
            ins.then_inc(s_sorted, 1)
            pe.wait_ge(s_slot, 1)
            pe.wait_ge(s_wl, 16 * (2 * KC + FC))
            expert_reg = [pe.alloc_register("expert_even"), pe.alloc_register("expert_odd")]

            def fetch_expert(n, u):
                at = expert_i[0:1, n:n + 1] if isinstance(n, int) else expert_i[0:1, bass.ds(n, 1)]
                pe.reg_load(expert_reg[u], at)

            def expert(u):
                return pe.snap(expert_reg[u], min_val=0, max_val=NE - 1)

            def rows_T(n, u):
                pe.wait_ge(s_xnn, n + 1)
                if not (isinstance(n, int) and n == 0):
                    pe.wait_ge(s_eT, n)
                for k in range(KC):
                    ins = pe.transpose(bank[0][:, k * P:(k + 1) * P], xn[u][:, k * P:(k + 1) * P], ident[:, :])
                ins.then_inc(s_eTps, 1)

            def hidden(w, bk, n, u, e):
                if w is W1:
                    pe.wait_ge(s_eT, n + 1)
                    if not (isinstance(n, int) and n < 2):
                        pe.wait_ge(s_hid, n - 1)
                for k in range(KC):
                    ins = pe.matmul(bk[:, 0:F], xsT[u][:, k, :], w[:, k, bass.ds(e * F, F)],
                                    start=(k == 0), stop=(k == KC - 1))
                ins.then_inc(s_h, 1)

            def hidden_T(n, u):
                pe.wait_ge(s_hid, n + 1)
                if not (isinstance(n, int) and n == 0):
                    pe.wait_ge(s_hT, n * 2)
                for k in range(FC):
                    m = P if k < FC - 1 else F_LAST
                    ins = pe.transpose(bank[5][0:m, k * P:(k + 1) * P], hid[u][:, k * P:k * P + m], ident[:, :])
                ins.then_inc(s_hTps, 1)

            def down(n, u, e):
                pe.wait_ge(s_hT, n * 2 + 2)
                if not (isinstance(n, int) and n < 2):
                    pe.wait_ge(s_yo, n - 1)
                for k in range(FC):
                    m = P if k < FC - 1 else F_LAST
                    ins = pe.matmul(bank[6 + u][:, 0:DM], hidT[u][0:m, k, :], W3[0:m, k, bass.ds(e * DM, DM)],
                                    start=(k == 0), stop=(k == FC - 1))
                ins.then_inc(s_yps, 1)

            def tile_step(n, u, more=True):
                e, e_before = expert(u), expert(1 - u)
                hidden(W1, bank[1 + u], n, u, e)
                hidden_T(n - 1, 1 - u)
                hidden(W2, bank[3 + u], n, u, e)
                if more:
                    fetch_expert(n + 1, 1 - u)
                    rows_T(n + 1, 1 - u)
                down(n - 1, 1 - u, e_before)

            fetch_expert(0, 0)
            rows_T(0, 0)
            rows_T(1, 1)
            hidden(W1, bank[1], 0, 0, expert(0))
            hidden(W2, bank[3], 0, 0, expert(0))
            fetch_expert(1, 1)
            tile_step(1, 1)
            tile_step(2, 0)
            with pe.Fori(0, (NT - 4) // 2) as i:
                tile_step(i * 2 + 3, 1)
                tile_step(i * 2 + 4, 0)
            tile_step(NT - 1, 1, more=False)
            hidden_T(NT - 1, 1)
            down(NT - 1, 1, expert(1))


def kernel(**inputs):
    import ml_dtypes
    import numpy as np
    import concourse.bacc as _bacc
    from concourse.bass_utils import run_bass_kernel_spmd as _run

    a = {k.replace("L0_", ""): np.asarray(v) for k, v in inputs.items()}
    f4 = np.float32

    def both(v):
        v = v.reshape((CG, 64) + v.shape[1:])
        v = np.moveaxis(v, 1, 0)
        return np.ascontiguousarray(np.concatenate([v, v], axis=0))

    w_in = np.ascontiguousarray(a["conv_in_proj_w"].T.reshape(KC, P, 2 * DI).transpose(1, 0, 2))
    xp = a["conv_x_proj_w"]
    w_xd = np.zeros((P, ND, CG, P), f4)
    w_dt = np.zeros((64, ND, CG, P), f4)
    for k in range(ND):
        for j in range(CG):
            for b in range(2):
                rows = slice(64 * b, 64 * b + 64)
                ch = slice(64 * j, 64 * j + 64)
                w_xd[rows, k, j, 32 * b:32 * b + R] = xp[k, 0:R, ch].T
                w_xd[rows, k, j, 64 + 16 * b:80 + 16 * b] = xp[k, R:R + NS, ch].T
                w_xd[rows, k, j, 96 + 16 * b:112 + 16 * b] = xp[k, R + NS:, ch].T
                w_dt[32 * b:32 * b + R, k, j, rows] = a["conv_dt_projs_w"][k, ch, :].T
                w_dt[32 * b + R, k, j, rows] = a["conv_dt_projs_b"][k, ch]
    bias_row = np.zeros((P, 1), f4)
    bias_row[[R, 32 + R]] = 1
    w_out = np.zeros((P, 2, DM), f4)
    w_out[:, 0] = a["conv_out_proj_w"][:, 0:P].T
    for b in range(2):
        w_out[64 * b:64 * b + 64, 1] = a["conv_out_proj_w"][:, P:].T
    sel = np.zeros((96, NS, P), ml_dtypes.bfloat16)
    for q in range(96):
        b, n = (q // 16) % 2, q % 16
        sel[q, n, 64 * b:64 * b + 64] = 1
    half_ones = np.zeros((P, P), f4)
    half_ones[0:64, 0:64] = 1.0 / DI
    half_ones[64:, 64:] = 1.0 / DI
    w3 = np.zeros((FC * P, NE * DM), f4)
    w3[0:F] = a["ffn_W3"].transpose(2, 0, 1).reshape(F, NE * DM)
    arrays = dict(
        x=np.ascontiguousarray(a["x"].reshape(NB, L, DM)),
        w_in=w_in,
        conv_w=both(a["conv_conv_w"].reshape(DI, 9)),
        conv_b=both(a["conv_conv_b"]),
        w_xd=w_xd, w_dt=w_dt,
        bias_row=bias_row,
        a_log=np.ascontiguousarray(both(a["conv_A_logs"].reshape(ND, DI, NS).transpose(1, 0, 2)).transpose(0, 2, 1, 3)),
        d_skip=np.ascontiguousarray(both(a["conv_Ds"].reshape(ND, DI).T).transpose(0, 2, 1)),
        ln_g=both(a["conv_out_norm_g"]), ln_b=both(a["conv_out_norm_b"]),
        w_out=w_out,
        w_gate=np.ascontiguousarray(a["ffn_Wg"].T.reshape(KC, P, NE).transpose(1, 0, 2)),
        b_gate=np.ascontiguousarray(a["ffn_bg"]),
        w1=np.ascontiguousarray(a["ffn_W1"].transpose(2, 0, 1).reshape(KC, P, NE * F)),
        w2=np.ascontiguousarray(a["ffn_W2"].transpose(2, 0, 1).reshape(KC, P, NE * F)),
        w3=w3.reshape(FC, P, NE * DM),
        sel=sel, ident_d=np.eye(P, dtype=f4), half_ones=half_ones,
        tri_d=np.triu(np.ones((P, P), f4), 1),
    )
    nc = _bacc.Bacc("TRN2", target_bir_lowering=False, num_devices=1)
    feed, aps = {}, {}
    for name, v in arrays.items():
        feed["in_" + name] = v
        aps[name] = nc.dram_tensor("in_" + name, v.shape, mybir.dt.from_np(v.dtype), kind="ExternalInput").ap()
    out = nc.dram_tensor("out_0", (TOK, DM), F32, kind="ExternalOutput").ap()
    build(nc, **aps, out=out)
    r = _run(nc, [feed], core_ids=[0])
    return r.results[0]["out_0"].reshape(NB, HH, WW, DM)
```
